# Optimizing a Trainium2 kernel written in Bass

```python
import numpy as np
import jax
import jax.numpy as jnp

def _softmax(x, axis=-1):
    return jax.nn.softmax(x, axis=axis)

def _gelu(x):
    return jax.nn.gelu(x, approximate=True)

def _silu(x):
    return jax.nn.silu(x)

def _sigmoid(x):
    return jax.nn.sigmoid(x)

def _layernorm(x, axis=-1, eps=1e-05):
    m = jnp.mean(x, axis=axis, keepdims=True)
    v = jnp.var(x, axis=axis, keepdims=True)
    return (x - m) / jnp.sqrt(v + eps)

def _scatter_add(tgt, idx, src, axis=0):
    return tgt.at[idx].add(src)

def _segment_sum(src, seg, n):
    return jax.ops.segment_sum(src, seg, n)
kernel_name = 'mk_seq_preln_d1_jaxref_r4_210f4a'

def setup_inputs(seed: int=0):
    np.random.seed(seed)
    _w = jnp.asarray

    def _L0_attn_setup():
        import jax, jax.numpy as jnp
        import numpy as np
        B, S, E, H = (2, 512, 256, 16)
        HD = E // H
        LAMBDA_INIT = 0.8
        EPS = 1e-06
        key = jax.random.key(seed)
        ks = jax.random.split(key, 8)
        return {'x': jax.random.normal(ks[0], (B, S, E), dtype=jnp.float32), 'w_qkv': jax.random.normal(ks[1], (E, 3 * E), dtype=jnp.float32) * E ** (-0.5), 'wo': jax.random.normal(ks[2], (E, E), dtype=jnp.float32) * E ** (-0.5), 'lambda_q1': jax.random.normal(ks[3], (HD,), dtype=jnp.float32) * 0.1, 'lambda_q2': jax.random.normal(ks[4], (HD,), dtype=jnp.float32) * 0.1, 'lambda_k1': jax.random.normal(ks[5], (HD,), dtype=jnp.float32) * 0.1, 'lambda_k2': jax.random.normal(ks[6], (HD,), dtype=jnp.float32) * 0.1, 'norm_w': jnp.ones((H, HD), dtype=jnp.float32)}
    _L0_attn_in = _L0_attn_setup()

    def _L0_ffn_setup():
        import jax, jax.numpy as jnp
        import numpy as np
        EMB = 256
        FF = 4 * EMB

        def _ternary(w):
            scale = jnp.maximum(jnp.mean(jnp.abs(w)), 1e-08)
            w_t = jnp.clip(jnp.round(w / scale), -1.0, 1.0)
            return w + jax.lax.stop_gradient(w_t - w)
        key = jax.random.key(seed)
        kx, k1, k2, kb1, kb2 = jax.random.split(key, 5)
        x = jax.random.normal(kx, (4, 512, EMB), dtype=jnp.float32)
        lim1 = 1.0 / np.sqrt(EMB)
        lim2 = 1.0 / np.sqrt(FF)
        W1 = jax.random.uniform(k1, (FF, EMB), jnp.float32, -lim1, lim1)
        b1 = jax.random.uniform(kb1, (FF,), jnp.float32, -lim1, lim1)
        W2 = jax.random.uniform(k2, (EMB, FF), jnp.float32, -lim2, lim2)
        b2 = jax.random.uniform(kb2, (EMB,), jnp.float32, -lim2, lim2)
        return {'x': x, 'W1': W1, 'b1': b1, 'W2': W2, 'b2': b2}
    _L0_ffn_in = _L0_ffn_setup()
    _d = {'L0_attn_x': _L0_attn_in['x'], 'L0_attn_w_qkv': _L0_attn_in['w_qkv'], 'L0_attn_wo': _L0_attn_in['wo'], 'L0_attn_lambda_q1': _L0_attn_in['lambda_q1'], 'L0_attn_lambda_q2': _L0_attn_in['lambda_q2'], 'L0_attn_lambda_k1': _L0_attn_in['lambda_k1'], 'L0_attn_lambda_k2': _L0_attn_in['lambda_k2'], 'L0_attn_norm_w': _L0_attn_in['norm_w'], 'L0_ffn_W1': _L0_ffn_in['W1'], 'L0_ffn_b1': _L0_ffn_in['b1'], 'L0_ffn_W2': _L0_ffn_in['W2'], 'L0_ffn_b2': _L0_ffn_in['b2']}
    _x0 = _d['L0_attn_x']
    _d['L0_attn_x'] = jax.random.normal(jax.random.fold_in(jax.random.key(seed), 1), (32, 512, 256), dtype=_x0.dtype)
    del _x0
    return _d

def reference(L0_attn_x, L0_attn_w_qkv, L0_attn_wo, L0_attn_lambda_q1, L0_attn_lambda_q2, L0_attn_lambda_k1, L0_attn_lambda_k2, L0_attn_norm_w, L0_ffn_W1, L0_ffn_b1, L0_ffn_W2, L0_ffn_b2):

    def _L0_attn_ref(x, w_qkv, wo, lambda_q1, lambda_q2, lambda_k1, lambda_k2, norm_w):
        import jax, jax.numpy as jnp
        import numpy as np
        B, S, E, H = (2, 512, 256, 16)
        HD = E // H
        LAMBDA_INIT = 0.8
        EPS = 1e-06
        b, s, e = x.shape
        qkv = x @ w_qkv
        q, k, v = jnp.split(qkv, 3, axis=-1)

        def to_heads(t):
            return t.reshape(b, s, H, HD).transpose(0, 2, 1, 3)
        q, k, v = (to_heads(q), to_heads(k), to_heads(v))
        q1, q2 = jnp.split(q, 2, axis=-1)
        k1, k2 = jnp.split(k, 2, axis=-1)
        scale = 1.0 / jnp.sqrt(jnp.asarray(HD, dtype=x.dtype))
        a1 = jax.nn.softmax(jnp.einsum('bhsd,bhtd->bhst', q1, k1) * scale, axis=-1)
        a2 = jax.nn.softmax(jnp.einsum('bhsd,bhtd->bhst', q2, k2) * scale, axis=-1)
        lam = jnp.exp(jnp.dot(lambda_q1, lambda_k1)) - jnp.exp(jnp.dot(lambda_q2, lambda_k2)) + LAMBDA_INIT
        a = a1 - lam * a2
        out = jnp.einsum('bhst,bhtd->bhsd', a, v)
        rms = jnp.sqrt(jnp.mean(out * out, axis=-1, keepdims=True) + EPS)
        out_n = out / rms * norm_w[None, :, None, :] * (1.0 - LAMBDA_INIT)
        out_cat = out_n.reshape(b, H * s, HD)
        out_final = out_cat.transpose(0, 2, 1).reshape(b, s, e)
        return out_final @ wo

    def _L0_ffn_ref(x, W1, b1, W2, b2):
        import jax, jax.numpy as jnp
        import numpy as np
        EMB = 256
        FF = 4 * EMB

        def _ternary(w):
            scale = jnp.maximum(jnp.mean(jnp.abs(w)), 1e-08)
            w_t = jnp.clip(jnp.round(w / scale), -1.0, 1.0)
            return w + jax.lax.stop_gradient(w_t - w)
        h = jnp.einsum('bsd,fd->bsf', x, _ternary(W1)) + b1
        h = jax.nn.gelu(h, approximate=False)
        out = jnp.einsum('bsf,df->bsd', h, _ternary(W2)) + b2
        return out
    x = L0_attn_x
    x = x + _L0_attn_ref(_layernorm(x, axis=-1), L0_attn_w_qkv, L0_attn_wo, L0_attn_lambda_q1, L0_attn_lambda_q2, L0_attn_lambda_k1, L0_attn_lambda_k2, L0_attn_norm_w)
    x = x + _L0_ffn_ref(_layernorm(x, axis=-1), L0_ffn_W1, L0_ffn_b1, L0_ffn_W2, L0_ffn_b2)
    return x

_drawn_inputs = setup_inputs


def setup_inputs(seed=0):
    import zlib

    import numpy as np

    out = dict(_drawn_inputs(seed))
    spreads = {'L0_attn_norm_w': (1.0, 0.2)}
    factors = {'L0_attn_lambda_q1': 8.0,
     'L0_attn_lambda_q2': 5.782,
     'L0_attn_lambda_k1': 4.767,
     'L0_attn_lambda_k2': 4.313,
     'L0_ffn_b1': 22.921,
     'L0_ffn_b2': 64.0}
    for name, (base, spread) in spreads.items():
        noise = np.random.default_rng([zlib.crc32(name.encode()), seed]).standard_normal(out[name].shape)
        drawn = base * np.exp(spread * noise) if base else spread * noise
        out[name] = jnp.asarray(drawn.astype(out[name].dtype))
    for name, factor in factors.items():
        out[name] = (out[name] * factor).astype(out[name].dtype)
    return out
```

```python
import concourse.bass as bass
from concourse import mybir
from contextlib import ExitStack

F32 = mybir.dt.float32
BF16 = mybir.dt.bfloat16
F16 = mybir.dt.float16
ALU = mybir.AluOpType
ACT = mybir.ActivationFunctionType
AX = mybir.AxisListType

P = 128
B, S, E, H = 32, 512, 256, 16
HD = E // H
QD = HD // 2
FF = 4 * E
NT = S // P
EC = E // P
FC = FF // P
UNITS, STEPS, MAPS = 8, 4, 4
SLOTS = UNITS * STEPS * MAPS
LAMBDA_INIT = 0.8
RMS_EPS = 1e-6
LN_EPS = 1e-5
SCORE_SCALE = HD ** -0.5
VW = 32
HALF = 64
Q_PART = (0, 0, 0, 1, 1, 2)
K_PART = (0, 1, 2, 0, 1, 0)
ROWS = QD * len(Q_PART)
MROWS = ROWS + 3
DMA = 16

XT_PE = (11, 15)
PROJ_PE = (22, 26, 30, 38, 42, 46)
XT_ACT = (12, 16)
PROJ_ACT = (24, 28, 32, 40, 44, 48)
SPLIT_DVE = (25, 29, 33, 41)
STATS1_DVE = (0, 1, 2, 3)
AGGR1_DVE = 5
NORM1_DVE = (8, 9)
NEG_PE = 2
NEG_DVE = 4
WO_PE = (16, 20)
X2_DVE = ((18, 19), (22, 23))
STATS2_DVE = (20, 21, 24, 25)
AGGR2_DVE = 26
NORM2_DVE = (30, 31)
HI_ACT = 33
X2T_PE = (36, 41)
X2T_DVE = (38, 43)
FFN_UNIT = 3
FFN2_PE = [52 + 2 * n for n in range(16)] + [86 + 2 * n for n in range(16)]
FFN2_DVE = (83, 118)
DVE_SET = 18
FFN_AT = FFN_UNIT * STEPS * MAPS


def score_bank(slot):
    return (slot if slot < FFN_AT else slot + 1) % 3


def ffn_bank(j):
    return (FFN_AT + 1 + j) % 3


def bass_diff_attention_ternary_ffn(nc, x_in, w_qkv, wo, lq1, lq2, lk1, lk2, norm_rows, w1t, b1c, w2t, b2r, out):
    scratch = nc.dram_tensor("qk_parts", [2, 2, 3, E, S], BF16, kind="Internal").ap()
    ctx = ExitStack()
    with ctx:
        def sb(name, shape, dt):
            return ctx.enter_context(nc.sbuf_tensor(name, shape, dt))

        def pb(name, shape, dt):
            return ctx.enter_context(nc.psum_tensor(name, shape, dt))

        def sem(name):
            return ctx.enter_context(nc.semaphore(name))

        q_rows = [sb(f"q_rows{p}", [P, H, S], BF16) for p in range(2)]
        k_rows = [sb(f"k_rows{p}", [P, H, S], BF16) for p in range(2)]
        vals = [sb(f"vals{p}", [P, NT, H, VW], F32) for p in range(2)]
        probs = sb("probs", [P, 2, MAPS, S], F32)
        wqkv_sb = sb("wqkv_sb", [P, EC, 3 * E], F32)
        wo_sb = sb("wo_sb", [P, EC, E], F32)
        w1_tern = sb("w1_tern", [P, EC, FF], F16)
        w2_tern = sb("w2_tern", [P, FC, E], F32)
        x_sb = sb("x_sb", [P, NT, E], F32)
        xres = sb("xres", [P, NT, E], F32)
        xn = sb("xn", [P, NT, E], F32)
        xnT = sb("xnT", [P, EC, S], F32)
        parts = sb("parts", [P, 2, 3, S], BF16)
        rest = sb("rest", [P, 2, S], F32)
        pv_sb = sb("pv_sb", [P, S], F32)
        heads_n = sb("heads_n", [P, EC, HD, H, 2], F32)
        x2 = sb("x2", [P, NT, E], F32)
        x2b = sb("x2b", [P, NT, E], F32)
        x2n = sb("x2n", [P, NT, E], F32)
        x2hl = sb("x2hl", [P, 2, NT, E], F16)
        x2T = sb("x2T", [P, 2, EC, S], F16)
        hT = sb("hT", [P, FC, S], F32)
        y_sb = sb("y_sb", [P, NT, E], F32)
        ident = sb("ident", [P, P], F32)
        ident_b = sb("ident_b", [P, P], BF16)
        ident_h = sb("ident_h", [P, P], F16)
        ones = sb("ones", [P, P], F32)
        b1_sb = sb("b1_sb", [P, FC], F32)
        b2_sb = sb("b2_sb", [P, E], F32)
        nw_raw = sb("nw_raw", [P, NT], F32)
        nw = sb("nw", [P, NT], F32)
        lam_in = sb("lam_in", [P, 4, QD * 2], F32)
        lam_pr = sb("lam_pr", [P, 2, QD * 2], F32)
        lam_dot = sb("lam_dot", [P, 2], F32)
        lam_exp = sb("lam_exp", [P, 2], F32)
        lam_neg = sb("lam_neg", [P, 1], F32)
        map_sign = sb("map_sign", [P, NT * MAPS], F32)
        half_pow = sb("half_pow", [P, NT * 2], F32)
        zero = sb("zero", [P, 1], F32)
        ln_eps = sb("ln_eps", [P, NT], F32)
        rms_eps = sb("rms_eps", [P, NT * 2], F32)
        wsum = sb("wsum", [P, 2], F32)
        wthr = sb("wthr", [P, 2, 2], F32)
        st1 = sb("st1", [P, NT, 6], F32)
        mv1 = sb("mv1", [P, NT, 2], F32)
        ve1 = sb("ve1", [P, NT], F32)
        rstd1 = sb("rstd1", [P, NT], F32)
        st2 = sb("st2", [P, NT, 6], F32)
        mv2 = sb("mv2", [P, NT, 2], F32)
        ve2 = sb("ve2", [P, NT], F32)
        rstd2 = sb("rstd2", [P, NT], F32)
        neg = sb("neg", [P, 2, NT * MAPS], F32)
        neg_r = sb("neg_r", [P, NT * MAPS], F32)
        neg_parts = sb("neg_parts", [P, NT * MAPS, 3], BF16)
        neg_rows = sb("neg_rows", [3 * MAPS, 2, S], BF16)
        den = sb("den", [P, NT * MAPS], F32)
        den_s = sb("den_s", [P, NT * MAPS], F32)
        pair = sb("pair", [P, NT * MAPS, HD], F32)
        head = sb("head", [P, NT * 2, HD], F32)
        head_sq = sb("head_sq", [P, NT * 2, HD], F32)
        ssq = sb("ssq", [P, NT * 2], F32)
        ms = sb("ms", [P, NT * 2], F32)
        rrms = sb("rrms", [P, NT * 2], F32)
        w1_raw = probs[:, 0, :, :].rearrange("p a s -> p (a s)").rearrange("p (c f) -> p c f", c=EC)
        w2_raw = probs[:, 1, :, :].rearrange("p a s -> p (a s)").rearrange("p (c f) -> p c f", c=FC)
        w_below = hT[:, 0:4, :].rearrange("p a s -> p (a s)")

        score_ps = [pb(f"score_ps{i}", [P, S], F32) for i in range(3)]
        max_ps = [pb(f"max_ps{i}", [P, S], F32) for i in range(2)]
        pv_ps = pb("pv_ps", [P, S], F32)
        x_ps = pb("x_ps", [P, S], F32)
        y_ps = pb("y_ps", [P, S], F32)
        neg_ps = x_ps[:, :].bitcast(BF16)
        x2T_ps = y_ps[:, :].bitcast(F16)

        s_const = sem("s_const")
        s_w = sem("s_w")
        s_x = sem("s_x")
        s_xres = sem("s_xres")
        s_parts_out = [sem("s_parts_out0"), sem("s_parts_out1")]
        s_q_rows = sem("s_q_rows")
        s_k_rows = sem("s_k_rows")
        s_neg_rows = sem("s_neg_rows")
        s_out = sem("s_out")
        s_pool_set = sem("s_pool_set")
        s_dve_set = sem("s_dve_set")
        s_lam_dot = sem("s_lam_dot")
        s_lam_exp = sem("s_lam_exp")
        s_wsum = sem("s_wsum")
        s_wtot = sem("s_wtot")
        s_xT_mm = sem("s_xT_mm")
        s_proj_mm = sem("s_proj_mm")
        s_max_mm = sem("s_max_mm")
        s_neg_mm = sem("s_neg_mm")
        s_score_mm = sem("s_score_mm")
        s_pv_mm = sem("s_pv_mm")
        s_oT_mm = sem("s_oT_mm")
        s_wo_mm = sem("s_wo_mm")
        s_x2T_mm = sem("s_x2T_mm")
        s_ffn1_mm = sem("s_ffn1_mm")
        s_ffn2_mm = sem("s_ffn2_mm")
        s_xT = sem("s_xT")
        s_h_part = sem("s_h_part")
        s_vals = sem("s_vals")
        s_exp = sem("s_exp")
        s_pv_sb = sem("s_pv_sb")
        s_gelu = sem("s_gelu")
        s_x2_hi = sem("s_x2_hi")
        s_st1 = sem("s_st1")
        s_mv1 = sem("s_mv1")
        s_xn = sem("s_xn")
        s_max = sem("s_max")
        s_rest = sem("s_rest")
        s_neg_sb = sem("s_neg_sb")
        s_den = sem("s_den")
        s_pair = sem("s_pair")
        s_head = sem("s_head")
        s_ssq = sem("s_ssq")
        s_x2 = sem("s_x2")
        s_st2 = sem("s_st2")
        s_mv2 = sem("s_mv2")
        s_x2n = sem("s_x2n")
        s_x2T = sem("s_x2T")
        s_y = sem("s_y")
        s_rstd1 = sem("s_rstd1")
        s_mid = sem("s_mid")
        s_parts = sem("s_parts")
        s_neg_chain = sem("s_neg_chain")
        s_neg_parts = sem("s_neg_parts")
        s_head_sq = sem("s_head_sq")
        s_rms_chain = sem("s_rms_chain")
        s_heads_n = sem("s_heads_n")
        s_rstd2 = sem("s_rstd2")
        s_ve1 = sem("s_ve1")
        s_ve2 = sem("s_ve2")
        s_x2_lo = sem("s_x2_lo")
        s_x2b = sem("s_x2b")

        def due(count):
            return not isinstance(count, int) or count > 0

        def frames(eng, frame):
            for b in (-1, 0, 1):
                frame(b, b, b % 2)
            with eng.Fori(0, (B - 4) // 2) as i:
                frame(i * 2 + 2, 2, 0)
                frame(i * 2 + 3, 3, 1)
            for b in (B - 2, B - 1, B):
                frame(b, b, b % 2)

        def projects(k):
            return k + 1 < B

        def attends(k):
            return 0 <= k < B

        def finishes(k):
            return k >= 1

        def has_max(k, u):
            return 0 <= k * UNITS + u + 2 < B * UNITS

        def has_neg(k, u):
            return 0 <= k * UNITS + u + 1 < B * UNITS

        def has_head(k, u):
            return 0 <= k * UNITS + u - 1 < B * UNITS

        def maxima_at(k, u):
            if not has_max(k, u):
                return [()] * FC, [()] * 16
            if u == FFN_UNIT and finishes(k):
                return [(j,) for j in range(FC)], [(8 + n // 2,) if n % 2 else () for n in range(16)]
            return [()] * FC, [(n,) for n in range(16)]

        block = ctx.enter_context(nc.Block())

        @block.sync
        def _(sp):
            sp.dma_start(wqkv_sb[:, :, :], w_qkv.rearrange("(c p) n -> p c n", p=P)).then_inc(s_const, DMA)
            sp.dma_start(wo_sb[:, :, :], wo.rearrange("(c p) n -> p c n", p=P)).then_inc(s_const, DMA)
            sp.dma_start(b1_sb[:, :], b1c).then_inc(s_const, DMA)
            sp.dma_start(b2_sb[:, :], b2r.partition_broadcast(P)).then_inc(s_const, DMA)
            sp.dma_start(nw_raw[:, :], norm_rows).then_inc(s_const, DMA)
            for n, v in enumerate((lq1, lk1, lq2, lk2)):
                sp.dma_start(lam_in[:, n, :], v.partition_broadcast(P)).then_inc(s_const, DMA)
            sp.dma_start(w1_raw, w1t.rearrange("(c p) f -> p c f", p=P)).then_inc(s_w, DMA)
            sp.dma_start(w2_raw, w2t.rearrange("(c p) f -> p c f", p=P)).then_inc(s_w, DMA)

            def frame(b, k, par):
                for u in range(UNITS):
                    if u == 0 and projects(k):
                        if due(b + 1):
                            sp.wait_ge(s_xn, b + 1)
                        sp.dma_start(x_sb[:, :, :], x_in[b + 1].rearrange("(t p) e -> p t e", p=P)).then_inc(s_x, DMA)
                    if projects(k):
                        qk = {2: 0, 3: 1}.get(u)
                        if qk is not None:
                            for ft in range(EC):
                                n = 2 * qk + ft
                                sp.wait_ge(s_h_part, (b + 1) * 4 + n + 1)
                                sp.wait_ge(s_parts, (b + 1) * 4 + n + 1)
                                sp.dma_start(scratch[1 - par, qk, :, ft * P:(ft + 1) * P, :].rearrange("a f s -> f a s"),
                                             parts[:, n % 2, :, :]).then_inc(s_parts_out[n % 2], DMA)
                            for n in range(2):
                                sp.wait_ge(s_parts_out[n], ((b + 1) * 2 + qk + 1) * DMA)
                            dst, order, done = ((q_rows[1 - par], Q_PART, s_q_rows), (k_rows[1 - par], K_PART, s_k_rows))[qk]
                            for r in range(2):
                                for row, part in enumerate(order):
                                    src = scratch[1 - par, qk, part, :, :].rearrange("(t r d) s -> r d t s", r=2, d=QD)
                                    at = r * HALF + row * QD
                                    sp.dma_start(dst[at:at + QD, :, :], src[r]).then_inc(done, DMA)
                    if has_neg(k, u):
                        g = (u + 1) % UNITS
                        n = b * UNITS + u + 1
                        sp.wait_ge(s_neg_sb, n + 1)
                        dst = q_rows[par if u + 1 < UNITS else 1 - par]
                        for i in range(MAPS):
                            at = (i % 2) * HALF + ROWS
                            sp.dma_start(dst[at:at + 3, 2 * g + i // 2, :], neg_rows[3 * i:3 * i + 3, (u + 1) % 2, :])\
                              .then_inc(s_neg_rows, DMA)
                    if u == 3 and attends(k):
                        if due(b * NT):
                            sp.wait_ge(s_x2, b * NT)
                        sp.dma_start(xres[:, :, :], x_in[b].rearrange("(t p) e -> p t e", p=P)).then_inc(s_xres, DMA)
                    if u == 5 and finishes(k):
                        sp.wait_ge(s_y, (b - 1) * 2 + 1)
                        sp.dma_start(out[b - 1, 0:2 * P, :].rearrange("(t p) e -> p t e", p=P), y_sb[:, 0:2, :]).then_inc(s_out, DMA)
                    if u == 7 and finishes(k):
                        sp.wait_ge(s_y, (b - 1) * 2 + 2)
                        sp.dma_start(out[b - 1, 2 * P:4 * P, :].rearrange("(t p) e -> p t e", p=P), y_sb[:, 2:4, :]).then_inc(s_out, DMA)

            frames(sp, frame)
            sp.wait_ge(s_out, B * 2 * DMA)

        @block.gpsimd
        def _(pool):
            for m in (ident, ident_b, ident_h):
                pool.memset(m[:, :], 0.0)
            pool.memset(ones[:, :], 1.0)
            pool.memset(half_pow[:, :], -0.5)
            pool.memset(zero[:, :], 0.0)
            pool.memset(ln_eps[:, :], LN_EPS)
            pool.memset(rms_eps[:, :], HD * RMS_EPS)
            for p in range(2):
                pool.memset(vals[p][:, :, :, :], 0.0)
            pool.memset(neg_parts[:, :, :], 0.0).then_inc(s_pool_set, 1)
            pool.wait_ge(s_pool_set, 1)
            for p in range(2):
                pool.memset(vals[p][:, :, :, HD:HD + 1], 1.0)
            for m in (ident, ident_b, ident_h):
                last = pool.affine_select(out=m[:, :], in_=m[:, :], compare_op=ALU.not_equal, fill=1.0,
                                          base=0, pattern=[[-1, P]], channel_multiplier=1)
            last.then_inc(s_pool_set, 1)
            pool.wait_ge(s_const, 9 * DMA)

            def rstd(mv, ve, r, moments_ready, ve_ready, rstd_ready, n):
                pool.wait_ge(moments_ready, n + 1)
                pool.tensor_tensor(ve[:, :], mv[:, :, 1], ln_eps[:, :], ALU.add).then_inc(ve_ready, 1)
                pool.wait_ge(ve_ready, n + 1)
                pool.tensor_tensor(r[:, :], ve[:, :], half_pow[:, 0:NT], ALU.pow).then_inc(rstd_ready, 1)

            def frame(b, k, par):
                for u in range(UNITS):
                    if has_head(k, u):
                        n = b * UNITS + u - 1
                        g = (u - 1) % UNITS
                        pool.wait_ge(s_head, n + 1)
                        pool.tensor_tensor(head_sq[:, :, :], head[:, :, :], head[:, :, :], ALU.mult).then_inc(s_head_sq, 1)
                        pool.wait_ge(s_ssq, n + 1)
                        pool.tensor_tensor(ms[:, :], ssq[:, :], rms_eps[:, :], ALU.add).then_inc(s_rms_chain, 1)
                        pool.wait_ge(s_rms_chain, 2 * n + 1)
                        pool.tensor_tensor(rrms[:, :], ms[:, :], half_pow[:, 0:NT * 2], ALU.pow).then_inc(s_rms_chain, 1)
                        pool.wait_ge(s_rms_chain, 2 * n + 2)
                        if g == 0:
                            if due((b if u else b - 1) * 2):
                                pool.wait_ge(s_wo_mm, (b if u else b - 1) * 2)
                        for f in range(2):
                            last = pool.tensor_tensor(
                                heads_n[:, :, :, 2 * g:2 * g + 2, f].rearrange("p c d h -> p c h d"),
                                head[:, f * 4:f * 4 + 4, :].rearrange("p (c h) d -> p c h d", h=2),
                                rrms[:, f * 4:f * 4 + 4].rearrange("p (c h) -> p c h", h=2).unsqueeze(3).broadcast_to([P, EC, 2, HD]),
                                ALU.mult)
                        last.then_inc(s_heads_n, 1)
                    if u == 0 and projects(k):
                        rstd(mv1, ve1, rstd1, s_mv1, s_ve1, s_rstd1, b + 1)
                    if u == 1 and finishes(k):
                        rstd(mv2, ve2, rstd2, s_mv2, s_ve2, s_rstd2, b - 1)
                    if u == 2 and finishes(k):
                        pool.wait_ge(s_x2n, b)
                        pool.wait_ge(s_x2_hi, b)
                        if due((b - 1) * 2):
                            pool.wait_ge(s_x2T_mm, (b - 1) * 2)
                        pool.tensor_tensor(x2hl[:, 1, :, :], x2n[:, :, :], x2hl[:, 0, :, :], ALU.subtract).then_inc(s_x2_lo, 1)
                        if due((b - 1) * 2):
                            pool.wait_ge(s_y, (b - 1) * 2)
                        pool.tensor_tensor(x2b[:, :, :], x2[:, :, :],
                                           b2_sb[:, :].unsqueeze(1).broadcast_to([P, NT, E]), ALU.add).then_inc(s_x2b, 1)
                    if projects(k) and u in (1, 2):
                        for ft in range(EC):
                            n = 2 * (u - 1) + ft
                            c = (b + 1) * 4 + n
                            pool.wait_ge(s_rest, c + 1)
                            pool.tensor_tensor(parts[:, n % 2, 1, :], rest[:, n % 2, :], zero[:, :].broadcast_to([P, S]), ALU.add).then_inc(s_mid, 1)
                            pool.wait_ge(s_mid, c + 1)
                            pool.tensor_tensor(parts[:, n % 2, 2, :], rest[:, n % 2, :], parts[:, n % 2, 1, :], ALU.subtract).then_inc(s_parts, 1)
                    if has_max(k, u):
                        n = b * UNITS + u + 2
                        pool.wait_ge(s_max, 16 * (n + 1))
                        if due(n):
                            pool.wait_ge(s_neg_mm, n)
                        src = neg[:, u % 2, :]
                        pool.tensor_tensor(neg_parts[:, :, 0], src, zero[:, :].broadcast_to([P, NT * MAPS]), ALU.add).then_inc(s_neg_chain, 1)
                        pool.wait_ge(s_neg_chain, 3 * n + 1)
                        pool.tensor_tensor(neg_r[:, :], src, neg_parts[:, :, 0], ALU.subtract).then_inc(s_neg_chain, 1)
                        pool.wait_ge(s_neg_chain, 3 * n + 2)
                        pool.tensor_tensor(neg_parts[:, :, 1], neg_r[:, :], zero[:, :].broadcast_to([P, NT * MAPS]), ALU.add).then_inc(s_neg_chain, 1)
                        pool.wait_ge(s_neg_chain, 3 * n + 3)
                        pool.tensor_tensor(neg_parts[:, :, 2], neg_r[:, :], neg_parts[:, :, 1], ALU.subtract).then_inc(s_neg_parts, 1)

            frames(pool, frame)

        @block.scalar
        def _(act):
            act.wait_ge(s_lam_dot, 2)
            act.activation(lam_exp[:, :], lam_dot[:, :], ACT.Exp).then_inc(s_lam_exp, 1)

            def frame(b, k, par):
                for slot in range(SLOTS):
                    u, kt, i = slot // 16, slot // 4 % 4, slot % 4
                    if slot == FFN_AT and finishes(k):
                        for j in range(FC):
                            act.wait_ge(s_ffn1_mm, (b - 1) * FC + j + 1)
                            if j == 0:
                                if due((b - 1) * 2):
                                    act.wait_ge(s_ffn2_mm, (b - 1) * 2)
                            act.activation(hT[:, j, :], score_ps[ffn_bank(j)][:, :], ACT.Gelu,
                                           bias=b1_sb[:, j:j + 1]).then_inc(s_gelu, 1)
                    if attends(k):
                        act.wait_ge(s_score_mm, b * SLOTS + slot + 1)
                        if i == 0:
                            if due((b * UNITS + u) * STEPS + kt - 1):
                                act.wait_ge(s_pv_mm, (b * UNITS + u) * STEPS + kt - 1)
                        act.activation(probs[:, kt % 2, i, :], score_ps[score_bank(slot)][:, :], ACT.Exp,
                                       scale=SCORE_SCALE).then_inc(s_exp, 1)
                    if kt == 0 and i == 2 and has_head(k, u):
                        n = b * UNITS + u - 1
                        act.wait_ge(s_pv_mm, (n + 1) * STEPS)
                        if due(n):
                            act.wait_ge(s_oT_mm, n)
                        act.activation(pv_sb[:, :], pv_ps[:, :], ACT.Copy).then_inc(s_pv_sb, 1)
                    if projects(k):
                        if slot in XT_ACT:
                            c = XT_ACT.index(slot)
                            act.wait_ge(s_xT_mm, (b + 1) * 2 + c + 1)
                            if due((b + 1) * 6):
                                act.wait_ge(s_proj_mm, (b + 1) * 6)
                            act.activation(xnT[:, c, :], x_ps[:, :], ACT.Copy).then_inc(s_xT, 1)
                        if slot in PROJ_ACT:
                            n = PROJ_ACT.index(slot)
                            act.wait_ge(s_proj_mm, (b + 1) * 6 + n + 1)
                            if n < 4:
                                if due(((b + 1) * 2 + n // 2) * DMA):
                                    act.wait_ge(s_parts_out[n % 2], ((b + 1) * 2 + n // 2) * DMA)
                                act.activation(parts[:, n % 2, 0, :], x_ps[:, :], ACT.Copy).then_inc(s_h_part, 1)
                            else:
                                t = 2 * (n - 4)
                                act.activation(vals[1 - par][:, t:t + 2, :, 0:HD].rearrange("p t h d -> p (t h) d"),
                                               x_ps[:, :].rearrange("p (t d) -> p t d", d=HD), ACT.Copy)\
                                   .then_inc(s_vals, 1)
                    if slot == HI_ACT and finishes(k):
                        act.wait_ge(s_x2n, b)
                        if due((b - 1) * 2):
                            act.wait_ge(s_x2T_mm, (b - 1) * 2)
                        if due(b - 1):
                            act.wait_ge(s_x2_lo, b - 1)
                        act.activation(x2hl[:, 0, :, :], x2n[:, :, :], ACT.Copy).then_inc(s_x2_hi, 1)

            frames(act, frame)

        @block.vector
        def _(dve):
            steps = [0]

            def link(ins):
                steps[0] += 1
                ins.then_inc(s_dve_set, 1)
                dve.wait_ge(s_dve_set, steps[0])

            dve.wait_ge(s_const, 9 * DMA)
            link(dve.tensor_tensor(lam_pr[:, :, :], lam_in[:, 0:4:2, :], lam_in[:, 1:4:2, :], ALU.mult))
            dve.tensor_reduce(lam_dot[:, :], lam_pr[:, :, :], AX.X, ALU.add).then_inc(s_lam_dot, 2)
            link(dve.memset(map_sign[:, :], 1.0))
            link(dve.tensor_scalar(nw[:, :], nw_raw[:, :], (1.0 - LAMBDA_INIT) * HD ** 0.5, None, ALU.mult))
            dve.wait_ge(s_lam_exp, 1)
            link(dve.tensor_tensor(lam_neg[:, :], lam_exp[:, 0:1], lam_exp[:, 1:2], ALU.subtract))
            link(dve.tensor_scalar(lam_neg[:, :], lam_neg[:, :], -1.0, -LAMBDA_INIT, ALU.mult, ALU.add))
            odd = map_sign[:, :].rearrange("p (n j) -> p n j", j=2)[:, :, 1]
            link(dve.tensor_scalar(odd, odd, lam_neg[:, 0:1], None, ALU.mult))
            for p in range(2):
                for r in (0, HALF):
                    link(dve.memset(k_rows[p][r + 32:r + HALF, :, :], 1.0))
            dve.wait_ge(s_w, 2 * DMA)
            for n, raw in enumerate((w1_raw, w2_raw)):
                dve.tensor_reduce(wsum[:, n:n + 1], raw, AX.XY, ALU.add, apply_absolute_value=True).then_inc(s_wsum, 1)
            dve.wait_ge(s_wtot, 1)
            for n in range(2):
                link(dve.tensor_scalar(wthr[:, 0, n:n + 1], y_ps[:, n:n + 1], 1.0 / (FF * E), 1e-8, ALU.mult, ALU.max))
            link(dve.tensor_scalar(wthr[:, 1, :], wthr[:, 0, :], -0.5, None, ALU.mult))
            link(dve.tensor_scalar(wthr[:, 0, :], wthr[:, 0, :], 0.5, None, ALU.mult))
            for n, (raw, tern) in enumerate(((w1_raw, w1_tern), (w2_raw, w2_tern))):
                a, b = raw.rearrange("p c f -> p (c f)"), tern[:, :, :].rearrange("p c f -> p (c f)")
                link(dve.tensor_scalar(w_below, a, wthr[:, 1, n:n + 1], None, ALU.is_lt))
                link(dve.scalar_tensor_tensor(b, a, wthr[:, 0, n:n + 1], w_below, ALU.is_gt, ALU.subtract))
            assert steps[0] == DVE_SET

            def frame(b, k, par):
                def maxima(u, which):
                    g = b * UNITS + u + 2
                    for m in which:
                        dve.wait_ge(s_max_mm, g * 16 + m + 1)
                        if m == 0:
                            if due(g - 1):
                                dve.wait_ge(s_neg_parts, g - 1)
                        dve.tensor_reduce(neg[:, u % 2, m:m + 1], max_ps[m % 2][:, :], AX.X, ALU.max, negate=True)\
                           .then_inc(s_max, 1)

                for slot in range(SLOTS):
                    u, kt, i = slot // 16, slot // 4 % 4, slot % 4
                    with_ffn, in_slots = maxima_at(k, u)
                    if slot == FFN_AT and finishes(k):
                        for j in range(FC):
                            maxima(u, with_ffn[j])
                    if slot == AGGR1_DVE and projects(k):
                        dve.wait_ge(s_st1, (b + 2) * NT)
                    if slot == AGGR2_DVE and finishes(k):
                        dve.wait_ge(s_st2, b * NT)
                    maxima(u, in_slots[slot % 16])
                    if kt == 0 and i == 3 and has_head(k, u):
                        n = b * UNITS + u - 1
                        sums = pv_ps[:, :].rearrange("p (n w) -> p n w", w=VW)
                        dve.wait_ge(s_oT_mm, n + 1)
                        dve.reciprocal(den[:, :], sums[:, :, HD]).then_inc(s_den, 1)
                        dve.wait_ge(s_den, 2 * n + 1)
                        dve.tensor_tensor(den_s[:, :], den[:, :], map_sign[:, :], ALU.mult).then_inc(s_den, 1)
                        dve.wait_ge(s_den, 2 * n + 2)
                        dve.tensor_tensor(pair[:, :, :], sums[:, :, 0:HD],
                                          den_s[:, :].unsqueeze(2).broadcast_to([P, NT * MAPS, HD]), ALU.mult).then_inc(s_pair, 1)
                    if kt == 1 and i == 0:
                        if has_neg(k, u):
                            n = b * UNITS + u + 1
                            dve.wait_ge(s_neg_mm, n + 1)
                            if due((n - 1) * MAPS * DMA):
                                dve.wait_ge(s_neg_rows, (n - 1) * MAPS * DMA)
                            dve.tensor_copy(neg_rows[:, (u + 1) % 2, :], neg_ps[0:3 * MAPS, 0:S])\
                               .then_inc(s_neg_sb, 1)
                        if has_head(k, u):
                            n = b * UNITS + u - 1
                            dve.wait_ge(s_pair, n + 1)
                            if due(n):
                                dve.wait_ge(s_heads_n, n)
                            two = pair[:, :, :].rearrange("p (n j) d -> p n j d", j=2)
                            dve.tensor_tensor(head[:, :, :], two[:, :, 0, :], two[:, :, 1, :], ALU.add).then_inc(s_head, 1)
                    if kt == 1 and i == 2 and has_head(k, u):
                        n = b * UNITS + u - 1
                        dve.wait_ge(s_head_sq, n + 1)
                        dve.tensor_reduce(ssq[:, :], head_sq[:, :, :], AX.X, ALU.add).then_inc(s_ssq, 1)
                    if projects(k):
                        a = b + 1
                        if slot in STATS1_DVE:
                            t = STATS1_DVE.index(slot)
                            dve.wait_ge(s_x, (a + 1) * DMA)
                            dve.bn_stats(st1[:, t, :], x_sb[:, t, :]).then_inc(s_st1, 1)
                        if slot == AGGR1_DVE:
                            for t in range(NT):
                                last = dve.bn_aggr(mv1[:, t, :], st1[:, t, :])
                            last.then_inc(s_mv1, 1)
                        if slot in NORM1_DVE:
                            dve.wait_ge(s_rstd1, a + 1)
                            if due(a * 2):
                                dve.wait_ge(s_xT_mm, a * 2)
                            t = 2 * NORM1_DVE.index(slot)
                            dve.tensor_scalar(xn[:, t, :], x_sb[:, t, :], mv1[:, t, 0:1], rstd1[:, t:t + 1], ALU.subtract, ALU.mult)
                            last = dve.tensor_scalar(xn[:, t + 1, :], x_sb[:, t + 1, :], mv1[:, t + 1, 0:1], rstd1[:, t + 1:t + 2],
                                                     ALU.subtract, ALU.mult)
                            if t:
                                last.then_inc(s_xn, 1)
                        if slot in SPLIT_DVE:
                            n = SPLIT_DVE.index(slot)
                            dve.wait_ge(s_h_part, a * 4 + n + 1)
                            if due(a * 4 + n - 1):
                                dve.wait_ge(s_parts, a * 4 + n - 1)
                            dve.tensor_tensor(rest[:, n % 2, :], x_ps[:, :], parts[:, n % 2, 0, :], ALU.subtract)\
                               .then_inc(s_rest, 1)
                    if finishes(k):
                        a = b - 1
                        for h in range(2):
                            if slot in X2_DVE[h]:
                                t = 2 * h + X2_DVE[h].index(slot)
                                dve.wait_ge(s_wo_mm, a * 2 + h + 1)
                                dve.wait_ge(s_xres, (a + 1) * DMA)
                                if due(a):
                                    dve.wait_ge(s_x2b, a)
                                dve.scalar_tensor_tensor(x2[:, t, :], y_ps[:, (t % 2) * E:(t % 2 + 1) * E], nw[:, t:t + 1],
                                                         xres[:, t, :], ALU.mult, ALU.add).then_inc(s_x2, 1)
                        if slot in STATS2_DVE:
                            t = STATS2_DVE.index(slot)
                            dve.wait_ge(s_x2, a * NT + t + 1)
                            dve.bn_stats(st2[:, t, :], x2[:, t, :]).then_inc(s_st2, 1)
                        if slot == AGGR2_DVE:
                            for t in range(NT):
                                last = dve.bn_aggr(mv2[:, t, :], st2[:, t, :])
                            last.then_inc(s_mv2, 1)
                        if slot in NORM2_DVE:
                            dve.wait_ge(s_rstd2, a + 1)
                            if due(a):
                                dve.wait_ge(s_x2_lo, a)
                            t = 2 * NORM2_DVE.index(slot)
                            dve.tensor_scalar(x2n[:, t, :], x2[:, t, :], mv2[:, t, 0:1], rstd2[:, t:t + 1], ALU.subtract, ALU.mult)
                            last = dve.tensor_scalar(x2n[:, t + 1, :], x2[:, t + 1, :], mv2[:, t + 1, 0:1], rstd2[:, t + 1:t + 2],
                                                     ALU.subtract, ALU.mult)
                            if t:
                                last.then_inc(s_x2n, 1)
                        if slot in X2T_DVE:
                            n = X2T_DVE.index(slot)
                            dve.wait_ge(s_x2T_mm, a * 2 + n + 1)
                            if due(a * FC):
                                dve.wait_ge(s_ffn1_mm, a * FC)
                            dve.tensor_copy(x2T[:, n, :, :].rearrange("p c s -> p (c s)"), x2T_ps)\
                               .then_inc(s_x2T, 1)
                        if slot in FFN2_DVE:
                            n = FFN2_DVE.index(slot)
                            dve.wait_ge(s_ffn2_mm, a * 2 + n + 1)
                            dve.wait_ge(s_x2b, a + 1)
                            if due(a * 2 * DMA):
                                dve.wait_ge(s_out, a * 2 * DMA)
                            dve.tensor_tensor(y_sb[:, 2 * n:2 * n + 2, :].rearrange("p t e -> p (t e)"), y_ps[:, :],
                                              x2b[:, 2 * n:2 * n + 2, :].rearrange("p t e -> p (t e)"), ALU.add)\
                               .then_inc(s_y, 1)

            frames(dve, frame)

        @block.tensor
        def _(pe):
            pe.wait_ge(s_pool_set, 2)
            pe.wait_ge(s_wsum, 2)
            pe.matmul(y_ps[:, 0:2], ones[:, :], wsum[:, :], start=True, stop=True).then_inc(s_wtot, 1)
            pe.wait_ge(s_dve_set, DVE_SET)
            pe.wait_ge(s_const, 9 * DMA)

            def frame(b, k, par):
                def maxima(u, which):
                    g = b * UNITS + u + 2
                    p = par if u + 2 < UNITS else 1 - par
                    for m in which:
                        qt, i = m // 4, m % 4
                        if u + 2 == UNITS and m == 0:
                            pe.wait_ge(s_q_rows, (b + 2) * 12 * DMA)
                            pe.wait_ge(s_k_rows, (b + 2) * 12 * DMA)
                        if due(g * 16 + m - 1):
                            pe.wait_ge(s_max, g * 16 + m - 1)
                        t, r = 2 * ((u + 2) % UNITS) + i // 2, (i % 2) * HALF
                        pe.matmul(max_ps[m % 2][:, :], q_rows[p][r:r + ROWS, t, qt * P:(qt + 1) * P],
                                  k_rows[p][r:r + ROWS, t, :], start=True, stop=True).then_inc(s_max_mm, 1)

                def scores(u, kt, i, slot):
                    if kt == 0 and i == 0:
                        pe.wait_ge(s_neg_rows, (b * UNITS + u + 1) * MAPS * DMA)
                    if finishes(k) and FFN_AT <= slot < FFN_AT + 3:
                        pe.wait_ge(s_gelu, (b - 1) * FC + (7, 8, 6)[slot - FFN_AT])
                    elif FFN_AT <= slot < FFN_AT + 3:
                        pe.wait_ge(s_exp, b * SLOTS + FFN_AT + (-1, 0, -2)[slot - FFN_AT])
                    else:
                        if due(b * SLOTS + slot - 2):
                            pe.wait_ge(s_exp, b * SLOTS + slot - 2)
                    t, r = 2 * u + i // 2, (i % 2) * HALF
                    pe.matmul(score_ps[score_bank(slot)][:, :], k_rows[par][r:r + ROWS + 3, t, kt * P:(kt + 1) * P],
                              q_rows[par][r:r + ROWS + 3, t, :], start=True, stop=True).then_inc(s_score_mm, 1)

                def value_sums(u, kt, batch, p):
                    n = batch * UNITS + u
                    if kt == 0:
                        if due(n):
                            pe.wait_ge(s_pair, n)
                        if u == 0:
                            pe.wait_ge(s_vals, (batch + 1) * 2)
                    pe.wait_ge(s_exp, (n * STEPS + kt + 1) * MAPS)
                    for i in range(MAPS):
                        last = pe.matmul(pv_ps[i * VW:(i + 1) * VW, :], vals[p][:, kt, 2 * u + i // 2, :],
                                         probs[:, kt % 2, i, :], start=(kt == 0), stop=(kt == STEPS - 1))
                    last.then_inc(s_pv_mm, 1)

                for slot in range(SLOTS):
                    u, kt, i = slot // 16, slot // 4 % 4, slot % 4
                    with_ffn, in_slots = maxima_at(k, u)
                    if slot == FFN_AT and finishes(k):
                        a = b - 1
                        pe.wait_ge(s_x2T, (a + 1) * 2)
                        for j in range(FC):
                            if j < 3:
                                pe.wait_ge(s_exp, b * SLOTS + (FFN_AT + (-1, 0, -2)[j] if attends(k) else 0))
                            else:
                                pe.wait_ge(s_gelu, a * FC + j - 2)
                            for c in range(EC):
                                for n in range(2):
                                    last = pe.matmul(score_ps[ffn_bank(j)][:, :], w1_tern[:, c, j * P:(j + 1) * P],
                                                     x2T[:, n, c, :], start=(c == 0 and n == 0), stop=(c == 1 and n == 1))
                            last.then_inc(s_ffn1_mm, 1)
                            maxima(u, with_ffn[j])
                    if attends(k):
                        scores(u, kt, i, slot)
                    maxima(u, in_slots[slot % 16])
                    if i == 1:
                        if kt and attends(k):
                            value_sums(u, kt - 1, b, par)
                        elif not kt and u and attends(k):
                            value_sums(u - 1, STEPS - 1, b, par)
                        elif not kt and not u and attends(k - 1):
                            value_sums(UNITS - 1, STEPS - 1, b - 1, 1 - par)
                    if kt == 0 and i == 3 and has_head(k, u):
                        pe.wait_ge(s_pv_sb, b * UNITS + u)
                        for t in range(NT):
                            last = pe.transpose(pv_ps[:, t * P:(t + 1) * P], pv_sb[:, t * P:(t + 1) * P], ident[:, :])
                        last.then_inc(s_oT_mm, 1)
                    if slot % 16 == NEG_PE and has_neg(k, u):
                        if due(b * UNITS + u + 1):
                            pe.wait_ge(s_neg_sb, b * UNITS + u + 1)
                        if projects(k) and u == 1:
                            pe.wait_ge(s_xT, (b + 2) * 2)
                        if projects(k) and u == 2:
                            pe.wait_ge(s_rest, (b + 1) * 4 + 3)
                        if projects(k) and (u == 3 or k < 0):
                            pe.wait_ge(s_vals, (b + 2) * 2)
                        pe.wait_ge(s_neg_parts, b * UNITS + u + 2)
                        for t in range(NT):
                            last = pe.transpose(neg_ps[0:3 * MAPS, t * P:(t + 1) * P],
                                                neg_parts[:, t * MAPS:(t + 1) * MAPS, :].rearrange("p i a -> p (i a)"), ident_b[:, :])
                        last.then_inc(s_neg_mm, 1)
                    if projects(k):
                        if slot in XT_PE:
                            c = XT_PE.index(slot)
                            if due(b * UNITS + 2):
                                pe.wait_ge(s_neg_sb, b * UNITS + 2)
                            if due((b + 1) * 2 + c):
                                pe.wait_ge(s_xT, (b + 1) * 2 + c)
                            pe.wait_ge(s_xn, b + 2)
                            for t in range(NT):
                                last = pe.transpose(x_ps[:, t * P:(t + 1) * P], xn[:, t, c * P:(c + 1) * P], ident[:, :])
                            last.then_inc(s_xT_mm, 1)
                        if slot in PROJ_PE:
                            n = PROJ_PE.index(slot)
                            if due(b * UNITS + (3 if n < 3 else 4)):
                                pe.wait_ge(s_neg_sb, b * UNITS + (3 if n < 3 else 4))
                            if due((b + 1) * 4 + min(n, 4)):
                                pe.wait_ge(s_rest, (b + 1) * 4 + min(n, 4))
                            if n == 5:
                                pe.wait_ge(s_vals, (b + 1) * 2 + 1)
                            if n == 0:
                                pe.wait_ge(s_xT, (b + 2) * 2)
                            if n < 4:
                                for c in range(EC):
                                    last = pe.matmul(x_ps[:, :], wqkv_sb[:, c, n * P:(n + 1) * P], xnT[:, c, :],
                                                     start=(c == 0), stop=(c == 1))
                            else:
                                for t in range(2):
                                    at = (2 * (n - 4) + t) * P
                                    for c in range(EC):
                                        last = pe.matmul(x_ps[:, t * E:(t + 1) * E], xnT[:, c, at:at + P],
                                                         wqkv_sb[:, c, 2 * E:3 * E], start=(c == 0), stop=(c == 1))
                            last.then_inc(s_proj_mm, 1)
                    if finishes(k):
                        a = b - 1
                        if slot in WO_PE:
                            h = WO_PE.index(slot)
                            if due(a * 2):
                                pe.wait_ge(s_y, a * 2)
                            if due(a * NT + 2 * h):
                                pe.wait_ge(s_x2, a * NT + 2 * h)
                            pe.wait_ge(s_heads_n, (a + 1) * UNITS)
                            by_row = heads_n[:, :, :, :, :].rearrange("p c d h f -> p c (d h f)")
                            for t in range(2):
                                at = (2 * h + t) * P
                                for c in range(EC):
                                    last = pe.matmul(y_ps[:, t * E:(t + 1) * E], by_row[:, c, at:at + P], wo_sb[:, c, :],
                                                     start=(c == 0), stop=(c == 1))
                            last.then_inc(s_wo_mm, 1)
                        if slot in X2T_PE:
                            n = X2T_PE.index(slot)
                            pe.wait_ge(s_x2, (a + 1) * NT)
                            if due(a * 2 + n):
                                pe.wait_ge(s_x2T, a * 2 + n)
                            pe.wait_ge((s_x2_hi, s_x2_lo)[n], a + 1)
                            for c in range(EC):
                                for t in range(NT):
                                    at = c * S + t * P
                                    last = pe.transpose(x2T_ps[:, at:at + P], x2hl[:, n, t, c * P:(c + 1) * P], ident_h[:, :])
                            last.then_inc(s_x2T_mm, 1)
                        if slot in FFN2_PE:
                            n = FFN2_PE.index(slot)
                            t, f = n // FC, n % FC
                            if n % 16 == 0:
                                pe.wait_ge(s_x2T, (a + 1) * 2)
                                if due(a * 2 + n // 16):
                                    pe.wait_ge(s_y, a * 2 + n // 16)
                                pe.wait_ge(s_gelu, (a + 1) * FC)
                            last = pe.matmul(y_ps[:, (t % 2) * E:(t % 2 + 1) * E], hT[:, f, t * P:(t + 1) * P], w2_tern[:, f, :],
                                             start=(f == 0), stop=(f == FC - 1))
                            if n % 16 == 15:
                                last.then_inc(s_ffn2_mm, 1)

            frames(pe, frame)


_INS = ["x", "w_qkv", "wo", "lq1", "lq2", "lk1", "lk2", "norm_rows", "w1t", "b1c", "w2t", "b2r"]


def kernel(L0_attn_x, L0_attn_w_qkv, L0_attn_wo, L0_attn_lambda_q1, L0_attn_lambda_q2, L0_attn_lambda_k1,
           L0_attn_lambda_k2, L0_attn_norm_w, L0_ffn_W1, L0_ffn_b1, L0_ffn_W2, L0_ffn_b2):
    import numpy as _np
    import concourse.bacc as _bacc
    from concourse import mybir as _mybir
    from concourse.bass_utils import run_bass_kernel_spmd as _run

    norm_w = _np.asarray(L0_attn_norm_w)
    by_row = _np.repeat(norm_w.T.reshape(-1), 2).reshape(NT, P).T
    laid = {
        "x": L0_attn_x, "w_qkv": L0_attn_w_qkv, "wo": L0_attn_wo,
        "lq1": L0_attn_lambda_q1, "lq2": L0_attn_lambda_q2, "lk1": L0_attn_lambda_k1, "lk2": L0_attn_lambda_k2,
        "norm_rows": by_row, "w1t": _np.asarray(L0_ffn_W1).T, "b1c": _np.asarray(L0_ffn_b1).reshape(FC, P).T,
        "w2t": _np.asarray(L0_ffn_W2).T, "b2r": L0_ffn_b2,
    }
    nc = _bacc.Bacc("TRN2", target_bir_lowering=False, num_devices=1)
    arrays, args = {}, []
    for name in _INS:
        a = _np.ascontiguousarray(laid[name])
        arrays[f"in_{name}"] = a
        args.append(nc.dram_tensor(f"in_{name}", a.shape, _mybir.dt.from_np(a.dtype), kind="ExternalInput").ap())
    args.append(nc.dram_tensor("out", (B, S, E), F32, kind="ExternalOutput").ap())
    bass_diff_attention_ternary_ffn(nc, *args)
    r = _run(nc, [arrays], core_ids=[0])
    return r.results[0]["out"]
```

```python
import numpy as np
import concourse.bass as bass
from concourse import mybir
from contextlib import ExitStack

F32 = mybir.dt.float32
BF16 = mybir.dt.bfloat16
F16 = mybir.dt.float16
ALU = mybir.AluOpType
ACT = mybir.ActivationFunctionType
AX = mybir.AxisListType

P = 128
B, S, E, H = 32, 512, 256, 16
HD = E // H
QD = HD // 2
FF = 4 * E
NT = S // P
EC = E // P
FC = FF // P
UNITS, STEPS, MAPS = 8, 4, 4
SLOTS = UNITS * STEPS * MAPS
LAMBDA_INIT = 0.8
RMS_EPS = 1e-6
LN_EPS = 1e-5
SCORE_SCALE = HD ** -0.5
VW = 32
HALF = 64
Q_PART = (0, 0, 0, 1, 1, 2)
K_PART = (0, 1, 2, 0, 1, 0)
ROWS = QD * len(Q_PART)
MROWS = ROWS + 3
DMA = 16
SCORE_MAP = (0, 2, 1, 3)
MAX_MAP = (1, 3, 0, 2)

STATS1_DVE, AGGR1_DVE, NORM1_DVE = (99, 102, 105, 108), 111, (118, 121)
FIRST_STATS1_DVE, FIRST_AGGR1_DVE, FIRST_NORM1_DVE = (0, 1, 2, 3), 5, (10, 11)
XT_PE = (14, 17)
XT_ACT = (15, 18)
NEG_PE, NEG_ACT = 5, 6
PROJ_PE = (25, 29, 42, 47, 58, 63)
PROJ_ACT = (27, 31, 44, 49, 60, 65)
WO_PE = (19, 24)
X2_DVE = ((21, 22), (25, 27))
STATS2_DVE = (23, 24, 29, 30)
AGGR2_DVE = 33
NORM2_DVE = (39, 42, 43, 45)
HI_ACT = (43, 46)
X2T_PE = (50, 57)
X2T_DVE = (51, 58)
FFN_UNIT = 4
LATE_TILES = (5, 6, 7)
H_HI_ACT, H_LO_DVE = (71, 75, 79), (72, 76, 80)
FFN2_PE = [82 + 2 * n for n in range(8)] + [101 + 3 * n for n in range(8)]
FFN2_DVE = (99, 125)
LAM_ACT, SETUP_DVE, WTOT_PE = 20, 12, 50
DVE_SET, CONST_LOADS = 17, 9
TWO_ONES = float(np.array([0x3F803F80], np.uint32).view(np.float32)[0])
FFN_AT = FFN_UNIT * STEPS * MAPS


def score_bank(slot):
    return (slot if slot < FFN_AT else slot + 1) % 3


def ffn_bank(j):
    return (FFN_AT + 1 + j) % 3


def bass_diff_attention_ternary_ffn(nc, x_in, w_qkv, wo, lq1, lq2, lk1, lk2, norm_rows, w1t, b1c, b1r, w2t, b2r, out):
    scratch = nc.dram_tensor("qk_parts", [2, 2, 3, E, S], BF16, kind="Internal").ap()
    ctx = ExitStack()
    with ctx:
        def sb(name, shape, dt):
            return ctx.enter_context(nc.sbuf_tensor(name, shape, dt))

        def pb(name, shape, dt):
            return ctx.enter_context(nc.psum_tensor(name, shape, dt))

        def sem(name):
            return ctx.enter_context(nc.semaphore(name))

        q_rows = [sb(f"q_rows{p}", [P, H, S], BF16) for p in range(2)]
        k_rows = [sb(f"k_rows{p}", [P, H, S], BF16) for p in range(2)]
        vals = [sb(f"vals{p}", [P, NT, H, VW], F32) for p in range(2)]
        probs = sb("probs", [P, 2, MAPS, S], F32)
        wqkv_sb = sb("wqkv_sb", [P, EC, 3 * E], F32)
        wo_sb = sb("wo_sb", [P, EC, E], F32)
        w1_tern = sb("w1_tern", [P, EC, FF], F16)
        w2_tern = sb("w2_tern", [P, FC, E], F16)
        x_sb = sb("x_sb", [P, NT, E], F32)
        xres = sb("xres", [P, NT, E], F32)
        xn = sb("xn", [P, NT, E], F32)
        xnT = sb("xnT", [P, EC, S], F32)
        parts = sb("parts", [P, 2, 3, S], BF16)
        qk_whole = sb("qk_whole", [P, 2, S], F32)
        pv_sb = sb("pv_sb", [P, S], F32)
        heads_n = sb("heads_n", [P, EC, HD, H, 2], F32)
        x2 = sb("x2", [P, NT, E], F32)
        x2b = sb("x2b", [P, NT, E], F32)
        x2n = sb("x2n", [P, NT, E], F32)
        x2hl = sb("x2hl", [P, 2, NT, E], F16)
        x2T = sb("x2T", [P, 2, EC, S], F16)
        hT = sb("hT", [P, FC, S], F32)
        h_hi = sb("h_hi", [P, FC, S], F16)
        h_lo = sb("h_lo", [P, FC, S], F16)
        ident = sb("ident", [P, P], F32)
        ident_b = sb("ident_b", [P, P], BF16)
        ident_h = sb("ident_h", [P, P], F16)
        b1_sb = sb("b1_sb", [P, FC], F32)
        b2_sb = sb("b2_sb", [P, E], F32)
        nw_raw = sb("nw_raw", [P, NT], F32)
        nw = sb("nw", [P, NT], F32)
        lam_in = sb("lam_in", [P, 4, QD * 2], F32)
        lam_pr = sb("lam_pr", [P, 2, QD * 2], F32)
        lam_dot = sb("lam_dot", [P, 2], F32)
        lam_exp = sb("lam_exp", [P, 2], F32)
        lam_neg = sb("lam_neg", [P, 1], F32)
        half_pow = sb("half_pow", [P, NT * 2], F32)
        zero = sb("zero", [P, 1], F32)
        ln_eps = sb("ln_eps", [P, NT], F32)
        rms_eps = sb("rms_eps", [P, NT * 2], F32)
        wsum = sb("wsum", [P, 2], F32)
        wthr = sb("wthr", [P, 2, 2], F32)
        h_bound = sb("h_bound", [P, 1], F32)
        sigma = sb("sigma", [P, 1], F32)
        sigma_inv = sb("sigma_inv", [P, 1], F32)
        st1 = sb("st1", [P, NT, 6], F32)
        mv1 = sb("mv1", [P, NT, 2], F32)
        ve1 = sb("ve1", [P, NT], F32)
        rstd1 = sb("rstd1", [P, NT], F32)
        st2 = sb("st2", [P, NT, 6], F32)
        mv2 = sb("mv2", [P, NT, 2], F32)
        ve2 = sb("ve2", [P, NT], F32)
        rstd2 = sb("rstd2", [P, NT], F32)
        neg = sb("neg", [P, 2, NT * MAPS], F32)
        neg_r = sb("neg_r", [P, NT * MAPS], F32)
        neg_parts = sb("neg_parts", [P, NT * MAPS, 3], BF16)
        neg_rows = sb("neg_rows", [3 * MAPS, 2, S], BF16)
        den = sb("den", [P, NT * MAPS], F32)
        pair = sb("pair", [P, NT * MAPS, HD], F32)
        head = sb("head", [P, NT * 2, HD], F32)
        head_sq = sb("head_sq", [P, NT * 2, HD], F32)
        ssq = sb("ssq", [P, NT * 2], F32)
        ms = sb("ms", [P, NT * 2], F32)
        rrms = sb("rrms", [P, NT * 2], F32)
        w1_raw = probs[:, 0, :, :].rearrange("p a s -> p (a s)").rearrange("p (c f) -> p c f", c=EC)
        w2_raw = probs[:, 1, :, :].rearrange("p a s -> p (a s)").rearrange("p (c f) -> p c f", c=FC)
        ones = hT[:, 4, 0:P]
        w_below = hT[:, 0:4, :].rearrange("p a s -> p (a s)")

        score_ps = [pb(f"score_ps{i}", [P, S], F32) for i in range(3)]
        max_ps = [pb(f"max_ps{i}", [P, S], F32) for i in range(2)]
        pv_ps = pb("pv_ps", [P, S], F32)
        x_ps = pb("x_ps", [P, S], F32)
        y_ps = pb("y_ps", [P, S], F32)
        neg_ps = x_ps[:, :].bitcast(BF16)
        x2T_ps = y_ps[:, :].bitcast(F16)

        s_const = sem("s_const")
        s_wqkv = sem("s_wqkv")
        s_w = sem("s_w")
        s_x = sem("s_x")
        s_xres = sem("s_xres")
        s_parts_out = [sem("s_parts_out0"), sem("s_parts_out1")]
        s_q_rows = sem("s_q_rows")
        s_k_rows = sem("s_k_rows")
        s_neg_rows = sem("s_neg_rows")
        s_out = sem("s_out")
        s_pool_set = sem("s_pool_set")
        s_dve_set = sem("s_dve_set")
        s_rows_set = sem("s_rows_set")
        s_lam_dot = sem("s_lam_dot")
        s_lam_exp = sem("s_lam_exp")
        s_wsum = sem("s_wsum")
        s_wtot = sem("s_wtot")
        s_xT_mm = sem("s_xT_mm")
        s_proj_mm = sem("s_proj_mm")
        s_max_mm = sem("s_max_mm")
        s_neg_mm = sem("s_neg_mm")
        s_score_mm = sem("s_score_mm")
        s_pv_mm = sem("s_pv_mm")
        s_oT_mm = sem("s_oT_mm")
        s_wo_mm = sem("s_wo_mm")
        s_x2T_mm = sem("s_x2T_mm")
        s_ffn1_mm = sem("s_ffn1_mm")
        s_ffn2_mm = sem("s_ffn2_mm")
        s_xT = sem("s_xT")
        s_h_part = sem("s_h_part")
        s_qk_whole = sem("s_qk_whole")
        s_vals = sem("s_vals")
        s_exp = sem("s_exp")
        s_pv_sb = sem("s_pv_sb")
        s_gelu = sem("s_gelu")
        s_h_hi = sem("s_h_hi")
        s_x2_hi = sem("s_x2_hi")
        s_st1 = sem("s_st1")
        s_mv1 = sem("s_mv1")
        s_xn = sem("s_xn")
        s_max = sem("s_max")
        s_neg_sb = sem("s_neg_sb")
        s_den = sem("s_den")
        s_pair = sem("s_pair")
        s_head = sem("s_head")
        s_ssq = sem("s_ssq")
        s_x2 = sem("s_x2")
        s_st2 = sem("s_st2")
        s_mv2 = sem("s_mv2")
        s_x2n = sem("s_x2n")
        s_x2T = sem("s_x2T")
        s_h_lo = sem("s_h_lo")
        s_y = sem("s_y")
        s_rstd1 = sem("s_rstd1")
        s_rest = sem("s_rest")
        s_mid = sem("s_mid")
        s_parts = sem("s_parts")
        s_neg_chain = sem("s_neg_chain")
        s_neg_parts = sem("s_neg_parts")
        s_head_sq = sem("s_head_sq")
        s_rms_chain = sem("s_rms_chain")
        s_heads_n = sem("s_heads_n")
        s_rstd2 = sem("s_rstd2")
        s_ve1 = sem("s_ve1")
        s_ve2 = sem("s_ve2")
        s_x2_lo = sem("s_x2_lo")
        s_x2b = sem("s_x2b")

        def due(count):
            return not isinstance(count, int) or count > 0

        def frames(eng, frame):
            for b in (-1, 0, 1):
                frame(b, b, b % 2)
            with eng.Fori(0, (B - 4) // 2) as i:
                frame(i * 2 + 2, 2, 0)
                frame(i * 2 + 3, 3, 1)
            for b in (B - 2, B - 1, B):
                frame(b, b, b % 2)

        def projects(k):
            return k + 1 < B

        def attends(k):
            return 0 <= k < B

        def finishes(k):
            return k >= 1

        def has_max(k, u):
            return 0 <= k * UNITS + u + 2 < B * UNITS

        def has_neg(k, u):
            return 0 <= k * UNITS + u + 1 < B * UNITS

        def has_head(k, u):
            return 0 <= k * UNITS + u - 1 < B * UNITS

        def maxima_at(k, u):
            if not has_max(k, u):
                return [()] * FC, [()] * 16
            if u == FFN_UNIT and finishes(k):
                return [(j,) for j in range(FC)], [(8 + n // 2,) if n % 2 else () for n in range(16)]
            return [()] * FC, [(n,) for n in range(16)]

        block = ctx.enter_context(nc.Block())

        @block.sync
        def _(sp):
            sp.dma_start(x_sb[:, :, :], x_in[0].rearrange("(t p) e -> p t e", p=P)).then_inc(s_x, DMA)
            sp.dma_start(wqkv_sb[:, :, :], w_qkv.rearrange("(c p) n -> p c n", p=P)).then_inc(s_wqkv, DMA)
            for n, v in enumerate((lq1, lk1, lq2, lk2)):
                sp.dma_start(lam_in[:, n, :], v.partition_broadcast(P)).then_inc(s_const, DMA)
            sp.dma_start(nw_raw[:, :], norm_rows).then_inc(s_const, DMA)
            sp.dma_start(x2b[:, :, :].rearrange("p t e -> p (t e)"), b1r.partition_broadcast(P)).then_inc(s_const, DMA)
            sp.dma_start(b1_sb[:, :], b1c).then_inc(s_const, DMA)
            sp.dma_start(b2_sb[:, :], b2r.partition_broadcast(P)).then_inc(s_const, DMA)
            sp.dma_start(wo_sb[:, :, :], wo.rearrange("(c p) n -> p c n", p=P)).then_inc(s_const, DMA)
            sp.dma_start(w1_raw, w1t.rearrange("(c p) f -> p c f", p=P)).then_inc(s_w, DMA)
            sp.dma_start(w2_raw, w2t.rearrange("(c p) f -> p c f", p=P)).then_inc(s_w, DMA)

            def frame(b, k, par):
                for u in range(UNITS):
                    if u == 1 and k + 2 < B:
                        sp.wait_ge(s_xn, b + 2)
                        sp.dma_start(x_sb[:, :, :], x_in[b + 2].rearrange("(t p) e -> p t e", p=P)).then_inc(s_x, DMA)
                    if has_neg(k, u):
                        g = (u + 1) % UNITS
                        n = b * UNITS + u + 1
                        sp.wait_ge(s_neg_sb, n + 1)
                        dst = q_rows[par if u + 1 < UNITS else 1 - par]
                        for i in range(MAPS):
                            at = (i % 2) * HALF + ROWS
                            sp.dma_start(dst[at:at + 3, 2 * g + i // 2, :], neg_rows[3 * i:3 * i + 3, (u + 1) % 2, :])\
                              .then_inc(s_neg_rows, DMA)
                    if projects(k):
                        qk = {2: 0, 4: 1}.get(u)
                        if qk is not None:
                            for ft in range(EC):
                                n = 2 * qk + ft
                                sp.wait_ge(s_h_part, (b + 1) * 4 + n + 1)
                                sp.wait_ge(s_parts, (b + 1) * 4 + n + 1)
                                sp.dma_start(scratch[1 - par, qk, :, ft * P:(ft + 1) * P, :].rearrange("a f s -> f a s"),
                                             parts[:, n % 2, :, :]).then_inc(s_parts_out[n % 2], DMA)
                            for n in range(2):
                                sp.wait_ge(s_parts_out[n], ((b + 1) * 2 + qk + 1) * DMA)
                            dst, order, done = ((q_rows[1 - par], Q_PART, s_q_rows), (k_rows[1 - par], K_PART, s_k_rows))[qk]
                            if k <= 0:
                                sp.wait_ge(s_rows_set, 2 * (k + 2))
                            for r in range(2):
                                for row, part in enumerate(order):
                                    src = scratch[1 - par, qk, part, :, :].rearrange("(t r d) s -> r d t s", r=2, d=QD)
                                    at = r * HALF + row * QD
                                    sp.dma_start(dst[at:at + QD, :, :], src[r]).then_inc(done, DMA)
                    if u == 3 and attends(k):
                        if due(b * NT):
                            sp.wait_ge(s_x2, b * NT)
                        sp.dma_start(xres[:, :, :], x_in[b].rearrange("(t p) e -> p t e", p=P)).then_inc(s_xres, DMA)
                    if u == 7 and finishes(k):
                        sp.wait_ge(s_y, (b - 1) * 2 + 1)
                        sp.dma_start(out[b - 1, 0:2 * P, :].rearrange("(t p) e -> p t e", p=P), x2b[:, 0:2, :]).then_inc(s_out, DMA)
                    if u == 7 and finishes(k):
                        sp.wait_ge(s_y, (b - 1) * 2 + 2)
                        sp.dma_start(out[b - 1, 2 * P:4 * P, :].rearrange("(t p) e -> p t e", p=P), x2b[:, 2:4, :]).then_inc(s_out, DMA)

            frames(sp, frame)
            sp.wait_ge(s_out, B * 2 * DMA)

        @block.gpsimd
        def _(pool):
            for m in (ident, ident_b, ident_h):
                pool.memset(m[:, :], 0.0)
            pool.memset(ones, 1.0)
            pool.memset(half_pow[:, :], -0.5)
            pool.memset(zero[:, :], 0.0)
            pool.memset(ln_eps[:, :], LN_EPS)
            pool.memset(rms_eps[:, :], HD * RMS_EPS)
            pool.memset(neg_parts[:, :, :], 0.0).then_inc(s_pool_set, 1)
            pool.wait_ge(s_pool_set, 1)
            for m in (ident, ident_b, ident_h):
                last = pool.affine_select(out=m[:, :], in_=m[:, :], compare_op=ALU.not_equal, fill=1.0,
                                          base=0, pattern=[[-1, P]], channel_multiplier=1)
            last.then_inc(s_pool_set, 1)

            def rstd(mv, ve, r, moments_ready, ve_ready, rstd_ready, n):
                pool.wait_ge(moments_ready, n + 1)
                pool.tensor_tensor(ve[:, :], mv[:, :, 1], ln_eps[:, :], ALU.add).then_inc(ve_ready, 1)
                pool.wait_ge(ve_ready, n + 1)
                pool.tensor_tensor(r[:, :], ve[:, :], half_pow[:, 0:NT], ALU.pow).then_inc(rstd_ready, 1)

            def split(b, n):
                c = (b + 1) * 4 + n
                pool.wait_ge(s_h_part, c + 1)
                pool.wait_ge(s_qk_whole, c + 1)
                pool.tensor_tensor(qk_whole[:, n % 2, :], qk_whole[:, n % 2, :], parts[:, n % 2, 0, :], ALU.subtract).then_inc(s_rest, 1)
                pool.wait_ge(s_rest, c + 1)
                pool.tensor_tensor(parts[:, n % 2, 1, :], qk_whole[:, n % 2, :], zero[:, :].broadcast_to([P, S]), ALU.add).then_inc(s_mid, 1)
                pool.wait_ge(s_mid, c + 1)
                pool.tensor_tensor(parts[:, n % 2, 2, :], qk_whole[:, n % 2, :], parts[:, n % 2, 1, :], ALU.subtract).then_inc(s_parts, 1)

            def frame(b, k, par):
                for u in range(UNITS):
                    if u == 0 and k < 0:
                        rstd(mv1, ve1, rstd1, s_mv1, s_ve1, s_rstd1, 0)
                        for p in range(2):
                            last = pool.memset(vals[p][:, :, :, :], 0.0)
                        last.then_inc(s_pool_set, 1)
                        pool.wait_ge(s_pool_set, 3)
                        for p in range(2):
                            last = pool.memset(vals[p][:, :, :, HD:HD + 1], 1.0)
                        last.then_inc(s_pool_set, 1)
                    if u == 7 and k + 2 < B:
                        rstd(mv1, ve1, rstd1, s_mv1, s_ve1, s_rstd1, b + 2)
                    if u == 3 and finishes(k):
                        pool.wait_ge(s_x2n, b * NT)
                        pool.wait_ge(s_x2_hi, b * 2)
                        if due((b - 1) * 2):
                            pool.wait_ge(s_x2T_mm, (b - 1) * 2)
                        pool.tensor_tensor(x2hl[:, 1, :, :], x2n[:, :, :], x2hl[:, 0, :, :], ALU.subtract).then_inc(s_x2_lo, 1)
                    if projects(k) and u in (2, 3):
                        split(b, u - 1)
                    if u == 5 and finishes(k):
                        if due((b - 1) * 2 * DMA):
                            pool.wait_ge(s_out, (b - 1) * 2 * DMA)
                        pool.wait_ge(s_x2, b * NT)
                        if k == 1:
                            pool.wait_ge(s_const, CONST_LOADS * DMA)
                        pool.tensor_tensor(x2b[:, :, :], x2[:, :, :],
                                           b2_sb[:, :].unsqueeze(1).broadcast_to([P, NT, E]), ALU.add).then_inc(s_x2b, 1)
                    if has_head(k, u):
                        n = b * UNITS + u - 1
                        g = (u - 1) % UNITS
                        pool.wait_ge(s_head, n + 1)
                        pool.tensor_tensor(head_sq[:, :, :], head[:, :, :], head[:, :, :], ALU.mult).then_inc(s_head_sq, 1)
                        pool.wait_ge(s_ssq, n + 1)
                        pool.tensor_tensor(ms[:, :], ssq[:, :], rms_eps[:, :], ALU.add).then_inc(s_rms_chain, 1)
                        pool.wait_ge(s_rms_chain, 2 * n + 1)
                        pool.tensor_tensor(rrms[:, :], ms[:, :], half_pow[:, 0:NT * 2], ALU.pow).then_inc(s_rms_chain, 1)
                        pool.wait_ge(s_rms_chain, 2 * n + 2)
                        if g == 0:
                            if due((b if u else b - 1) * 2):
                                pool.wait_ge(s_wo_mm, (b if u else b - 1) * 2)
                        for f in range(2):
                            last = pool.tensor_tensor(
                                heads_n[:, :, :, 2 * g:2 * g + 2, f].rearrange("p c d h -> p c h d"),
                                head[:, f * 4:f * 4 + 4, :].rearrange("p (c h) d -> p c h d", h=2),
                                rrms[:, f * 4:f * 4 + 4].rearrange("p (c h) -> p c h", h=2).unsqueeze(3).broadcast_to([P, EC, 2, HD]),
                                ALU.mult)
                        last.then_inc(s_heads_n, 1)
                    if projects(k) and u in (1, 3):
                        split(b, 0 if u == 1 else 3)
                    if u == 1 and finishes(k):
                        rstd(mv2, ve2, rstd2, s_mv2, s_ve2, s_rstd2, b - 1)
                    if has_max(k, u):
                        n = b * UNITS + u + 2
                        pool.wait_ge(s_max, 16 * (n + 1))
                        if due(n):
                            pool.wait_ge(s_neg_mm, n)
                        src = neg[:, u % 2, :]
                        pool.tensor_tensor(neg_parts[:, :, 0], src, zero[:, :].broadcast_to([P, NT * MAPS]), ALU.add).then_inc(s_neg_chain, 1)
                        pool.wait_ge(s_neg_chain, 3 * n + 1)
                        pool.tensor_tensor(neg_r[:, :], src, neg_parts[:, :, 0], ALU.subtract).then_inc(s_neg_chain, 1)
                        pool.wait_ge(s_neg_chain, 3 * n + 2)
                        pool.tensor_tensor(neg_parts[:, :, 1], neg_r[:, :], zero[:, :].broadcast_to([P, NT * MAPS]), ALU.add).then_inc(s_neg_chain, 1)
                        pool.wait_ge(s_neg_chain, 3 * n + 3)
                        pool.tensor_tensor(neg_parts[:, :, 2], neg_r[:, :], neg_parts[:, :, 1], ALU.subtract).then_inc(s_neg_parts, 1)

            frames(pool, frame)

        @block.scalar
        def _(act):
            def high_half(a, j):
                act.wait_ge(s_gelu, a * FC + j + 1)
                act.activation(h_hi[:, j, :], hT[:, j, :], ACT.Copy, scale=sigma[:, 0:1]).then_inc(s_h_hi, 1)

            def frame(b, k, par):
                for slot in range(SLOTS):
                    u, kt, i = slot // 16, slot // 4 % 4, slot % 4
                    if k < 0 and slot == LAM_ACT:
                        act.wait_ge(s_lam_dot, 2)
                        act.activation(lam_exp[:, :], lam_dot[:, :], ACT.Exp).then_inc(s_lam_exp, 1)
                    if slot == FFN_AT and finishes(k):
                        if k == 1:
                            act.wait_ge(s_const, CONST_LOADS * DMA)
                        for j in range(FC):
                            act.wait_ge(s_ffn1_mm, (b - 1) * FC + j + 1)
                            if j == 0:
                                if due((b - 1) * 2):
                                    act.wait_ge(s_ffn2_mm, (b - 1) * 2)
                            act.activation(hT[:, j, :], score_ps[ffn_bank(j)][:, :], ACT.Gelu,
                                           bias=b1_sb[:, j:j + 1]).then_inc(s_gelu, 1)
                            if 0 < j <= LATE_TILES[0]:
                                high_half(b - 1, j - 1)
                    if attends(k):
                        act.wait_ge(s_score_mm, b * SLOTS + slot + 1)
                        if i == 0:
                            if due((b * UNITS + u) * STEPS + kt - 1):
                                act.wait_ge(s_pv_mm, (b * UNITS + u) * STEPS + kt - 1)
                        act.activation(probs[:, kt % 2, SCORE_MAP[i], :], score_ps[score_bank(slot)][:, :], ACT.Exp,
                                       scale=SCORE_SCALE).then_inc(s_exp, 1)
                    if kt == 0 and i == 1 and has_head(k, u):
                        n = b * UNITS + u - 1
                        act.wait_ge(s_pv_mm, (n + 1) * STEPS)
                        if due(n):
                            act.wait_ge(s_oT_mm, n)
                        act.activation(pv_sb[:, :], pv_ps[:, :], ACT.Copy).then_inc(s_pv_sb, 1)
                    if slot % 16 == NEG_ACT and has_neg(k, u):
                        n = b * UNITS + u + 1
                        act.wait_ge(s_neg_mm, n + 1)
                        if due((n - 1) * MAPS * DMA):
                            act.wait_ge(s_neg_rows, (n - 1) * MAPS * DMA)
                        act.activation(neg_rows[:, (u + 1) % 2, :], neg_ps[0:3 * MAPS, 0:S], ACT.Copy).then_inc(s_neg_sb, 1)
                    if projects(k):
                        if slot in XT_ACT:
                            c = XT_ACT.index(slot)
                            act.wait_ge(s_xT_mm, (b + 1) * 2 + c + 1)
                            if due((b + 1) * 6):
                                act.wait_ge(s_proj_mm, (b + 1) * 6)
                            act.activation(xnT[:, c, :], x_ps[:, :], ACT.Copy).then_inc(s_xT, 1)
                        if slot in PROJ_ACT:
                            n = PROJ_ACT.index(slot)
                            act.wait_ge(s_proj_mm, (b + 1) * 6 + n + 1)
                            if n < 4:
                                if due(((b + 1) * 2 + n // 2) * DMA):
                                    act.wait_ge(s_parts_out[n % 2], ((b + 1) * 2 + n // 2) * DMA)
                                act.activation(parts[:, n % 2, 0, :], x_ps[:, :], ACT.Copy).then_inc(s_h_part, 1)
                                if due((b + 1) * 4 + n - 1):
                                    act.wait_ge(s_parts, (b + 1) * 4 + n - 1)
                                act.activation(qk_whole[:, n % 2, :], x_ps[:, :], ACT.Copy).then_inc(s_qk_whole, 1)
                            else:
                                t = 2 * (n - 4)
                                if k < 0:
                                    act.wait_ge(s_pool_set, 4)
                                act.activation(vals[1 - par][:, t:t + 2, :, 0:HD].rearrange("p t h d -> p (t h) d"),
                                               x_ps[:, :].rearrange("p (t d) -> p t d", d=HD), ACT.Copy)\
                                   .then_inc(s_vals, 1)
                    if slot in H_HI_ACT and finishes(k):
                        high_half(b - 1, LATE_TILES[H_HI_ACT.index(slot)])
                    if slot in HI_ACT and finishes(k):
                        h = HI_ACT.index(slot)
                        act.wait_ge(s_x2n, (b - 1) * NT + 2 * h + 2)
                        if due((b - 1) * 2):
                            act.wait_ge(s_x2T_mm, (b - 1) * 2)
                        if due(b - 1):
                            act.wait_ge(s_x2_lo, b - 1)
                        act.activation(x2hl[:, 0, 2 * h:2 * h + 2, :], x2n[:, 2 * h:2 * h + 2, :], ACT.Copy).then_inc(s_x2_hi, 1)

            frames(act, frame)

        @block.vector
        def _(dve):
            steps = [0]

            def link(ins):
                steps[0] += 1
                ins.then_inc(s_dve_set, 1)
                dve.wait_ge(s_dve_set, steps[0])

            def set_up():
                dve.wait_ge(s_const, CONST_LOADS * DMA)
                link(dve.tensor_tensor(lam_pr[:, :, :], lam_in[:, 0:4:2, :], lam_in[:, 1:4:2, :], ALU.mult))
                dve.tensor_reduce(lam_dot[:, :], lam_pr[:, :, :], AX.X, ALU.add).then_inc(s_lam_dot, 2)
                link(dve.tensor_scalar(nw[:, :], nw_raw[:, :], (1.0 - LAMBDA_INIT) * HD ** 0.5, None, ALU.mult))
                for p in range(2):
                    for rows, value in ((q_rows[p], 0.0), (k_rows[p], TWO_ONES)):
                        dve.memset(rows[:, :, :].rearrange("p t s -> p (t s)").bitcast(F32), value).then_inc(s_rows_set, 1)
                dve.wait_ge(s_lam_exp, 1)
                link(dve.tensor_tensor(lam_neg[:, :], lam_exp[:, 0:1], lam_exp[:, 1:2], ALU.subtract))
                link(dve.tensor_scalar(lam_neg[:, :], lam_neg[:, :], -1.0, -LAMBDA_INIT, ALU.mult, ALU.add))
                link(dve.tensor_reduce(h_bound[:, :], x2b[:, :, :], AX.XY, ALU.max, apply_absolute_value=True))
                link(dve.tensor_scalar(h_bound[:, :], h_bound[:, :], float(E), None, ALU.add))
                link(dve.tensor_scalar(h_bound[:, :].bitcast(mybir.dt.uint32), h_bound[:, :].bitcast(mybir.dt.uint32), 0x7F800000, None,
                                       ALU.bitwise_and))
                link(dve.tensor_scalar(sigma_inv[:, :], h_bound[:, :], 2.0 ** -14, None, ALU.mult))
                link(dve.reciprocal(sigma[:, :], sigma_inv[:, :]))
                dve.wait_ge(s_w, 2 * DMA)
                for n, raw in enumerate((w1_raw, w2_raw)):
                    dve.tensor_reduce(wsum[:, n:n + 1], raw, AX.XY, ALU.add, apply_absolute_value=True).then_inc(s_wsum, 1)
                dve.wait_ge(s_wtot, 1)
                for n in range(2):
                    link(dve.tensor_scalar(wthr[:, 0, n:n + 1], y_ps[:, n:n + 1], 1.0 / (FF * E), 1e-8, ALU.mult, ALU.max))
                link(dve.tensor_scalar(wthr[:, 1, :], wthr[:, 0, :], -0.5, None, ALU.mult))
                link(dve.tensor_scalar(wthr[:, 0, :], wthr[:, 0, :], 0.5, None, ALU.mult))
                for n, (raw, tern) in enumerate(((w1_raw, w1_tern), (w2_raw, w2_tern))):
                    a, b = raw.rearrange("p c f -> p (c f)"), tern[:, :, :].rearrange("p c f -> p (c f)")
                    link(dve.tensor_scalar(w_below, a, wthr[:, 1, n:n + 1], None, ALU.is_lt))
                    link(dve.scalar_tensor_tensor(b, a, wthr[:, 0, n:n + 1], w_below, ALU.is_gt, ALU.subtract))
                assert steps[0] == DVE_SET

            def frame(b, k, par):
                def maxima(u, which):
                    g = b * UNITS + u + 2
                    for m in which:
                        dve.wait_ge(s_max_mm, g * 16 + m + 1)
                        if m == 0:
                            if due(g - 1):
                                dve.wait_ge(s_neg_parts, g - 1)
                        at = m // 4 * MAPS + MAX_MAP[m % 4]
                        dve.tensor_reduce(neg[:, u % 2, at:at + 1], max_ps[m % 2][:, :], AX.X, ALU.max, negate=True)\
                           .then_inc(s_max, 1)

                def low_half(a, j):
                    dve.wait_ge(s_h_hi, a * FC + j + 1)
                    if j == 0 and due(a * 2):
                        dve.wait_ge(s_ffn2_mm, a * 2)
                    dve.scalar_tensor_tensor(h_lo[:, j, :], hT[:, j, :], sigma[:, 0:1], h_hi[:, j, :],
                                             ALU.mult, ALU.subtract).then_inc(s_h_lo, 1)

                def layernorm1(a, slot, stats_at, aggr_at, norm_at):
                    if slot in stats_at:
                        t = stats_at.index(slot)
                        dve.wait_ge(s_x, (a + 1) * DMA)
                        dve.bn_stats(st1[:, t, :], x_sb[:, t, :]).then_inc(s_st1, 1)
                    if slot == aggr_at:
                        if k < 0:
                            dve.wait_ge(s_st1, (a + 1) * NT)
                        for t in range(NT):
                            last = dve.bn_aggr(mv1[:, t, :], st1[:, t, :])
                        last.then_inc(s_mv1, 1)
                    if slot in norm_at:
                        dve.wait_ge(s_rstd1, a + 1)
                        if due(a * 2):
                            dve.wait_ge(s_xT_mm, a * 2)
                        t = 2 * norm_at.index(slot)
                        dve.tensor_scalar(xn[:, t, :], x_sb[:, t, :], mv1[:, t, 0:1], rstd1[:, t:t + 1], ALU.subtract, ALU.mult)
                        last = dve.tensor_scalar(xn[:, t + 1, :], x_sb[:, t + 1, :], mv1[:, t + 1, 0:1], rstd1[:, t + 1:t + 2],
                                                 ALU.subtract, ALU.mult)
                        if t:
                            last.then_inc(s_xn, 1)

                for slot in range(SLOTS):
                    u, kt, i = slot // 16, slot // 4 % 4, slot % 4
                    with_ffn, in_slots = maxima_at(k, u)
                    if slot == FFN_AT and finishes(k):
                        for j in range(FC):
                            maxima(u, with_ffn[j])
                            if 2 <= j < LATE_TILES[0] + 2:
                                low_half(b - 1, j - 2)
                    if slot == AGGR1_DVE and k + 2 < B:
                        dve.wait_ge(s_st1, (b + 3) * NT)
                    if slot == AGGR2_DVE and finishes(k):
                        dve.wait_ge(s_st2, b * NT)
                    maxima(u, in_slots[slot % 16])
                    if kt == 1 and i == 0 and has_head(k, u):
                        n = b * UNITS + u - 1
                        sums = pv_ps[:, :].rearrange("p (n w) -> p n w", w=VW)
                        dve.wait_ge(s_oT_mm, n + 1)
                        dve.reciprocal(den[:, :], sums[:, :, HD]).then_inc(s_den, 1)
                        dve.wait_ge(s_den, n + 1)
                        dve.tensor_tensor(pair[:, :, :], sums[:, :, 0:HD],
                                          den[:, :].unsqueeze(2).broadcast_to([P, NT * MAPS, HD]), ALU.mult).then_inc(s_pair, 1)
                    if kt == 1 and i == 1 and has_head(k, u):
                        n = b * UNITS + u - 1
                        dve.wait_ge(s_pair, n + 1)
                        if due(n):
                            dve.wait_ge(s_heads_n, n)
                        two = pair[:, :, :].rearrange("p (n j) d -> p n j d", j=2)
                        dve.scalar_tensor_tensor(head[:, :, :], two[:, :, 1, :], lam_neg[:, 0:1], two[:, :, 0, :],
                                                 ALU.mult, ALU.add).then_inc(s_head, 1)
                    if kt == 2 and i == 2 and has_head(k, u):
                        n = b * UNITS + u - 1
                        dve.wait_ge(s_head_sq, n + 1)
                        dve.tensor_reduce(ssq[:, :], head_sq[:, :, :], AX.X, ALU.add).then_inc(s_ssq, 1)
                    if k < 0:
                        layernorm1(0, slot, FIRST_STATS1_DVE, FIRST_AGGR1_DVE, FIRST_NORM1_DVE)
                        if slot == SETUP_DVE:
                            set_up()
                    if k + 2 < B:
                        layernorm1(b + 2, slot, STATS1_DVE, AGGR1_DVE, NORM1_DVE)
                    if finishes(k):
                        a = b - 1
                        for h in range(2):
                            if slot in X2_DVE[h]:
                                t = 2 * h + X2_DVE[h].index(slot)
                                dve.wait_ge(s_wo_mm, a * 2 + h + 1)
                                dve.wait_ge(s_xres, (a + 1) * DMA)
                                if due(a):
                                    dve.wait_ge(s_x2b, a)
                                dve.scalar_tensor_tensor(x2[:, t, :], y_ps[:, (t % 2) * E:(t % 2 + 1) * E], nw[:, t:t + 1],
                                                         xres[:, t, :], ALU.mult, ALU.add).then_inc(s_x2, 1)
                        if slot in STATS2_DVE:
                            t = STATS2_DVE.index(slot)
                            dve.wait_ge(s_x2, a * NT + t + 1)
                            dve.bn_stats(st2[:, t, :], x2[:, t, :]).then_inc(s_st2, 1)
                        if slot == AGGR2_DVE:
                            for t in range(NT):
                                last = dve.bn_aggr(mv2[:, t, :], st2[:, t, :])
                            last.then_inc(s_mv2, 1)
                        if slot in NORM2_DVE:
                            dve.wait_ge(s_rstd2, a + 1)
                            if due(a):
                                dve.wait_ge(s_x2_lo, a)
                            t = NORM2_DVE.index(slot)
                            dve.tensor_scalar(x2n[:, t, :], x2[:, t, :], mv2[:, t, 0:1], rstd2[:, t:t + 1], ALU.subtract, ALU.mult)\
                               .then_inc(s_x2n, 1)
                        if slot in X2T_DVE:
                            n = X2T_DVE.index(slot)
                            dve.wait_ge(s_x2T_mm, a * 2 + n + 1)
                            if due(a * FC):
                                dve.wait_ge(s_ffn1_mm, a * FC)
                            dve.tensor_copy(x2T[:, n, :, :].rearrange("p c s -> p (c s)"), x2T_ps)\
                               .then_inc(s_x2T, 1)
                        if slot in H_LO_DVE:
                            low_half(a, LATE_TILES[H_LO_DVE.index(slot)])
                        if slot in FFN2_DVE:
                            n = FFN2_DVE.index(slot)
                            dve.wait_ge(s_ffn2_mm, a * 2 + n + 1)
                            dve.wait_ge(s_x2b, a + 1)
                            half = x2b[:, 2 * n:2 * n + 2, :].rearrange("p t e -> p (t e)")
                            dve.scalar_tensor_tensor(half, y_ps[:, :], sigma_inv[:, 0:1], half, ALU.mult, ALU.add).then_inc(s_y, 1)

            frames(dve, frame)

        @block.tensor
        def _(pe):
            pe.wait_ge(s_pool_set, 2)
            def frame(b, k, par):
                def maxima(u, which):
                    g = b * UNITS + u + 2
                    p = par if u + 2 < UNITS else 1 - par
                    for m in which:
                        qt, i = m // 4, MAX_MAP[m % 4]
                        if u + 2 == UNITS and m == 0:
                            pe.wait_ge(s_q_rows, (b + 2) * 12 * DMA)
                            pe.wait_ge(s_k_rows, (b + 2) * 12 * DMA)
                        if due(g * 16 + m - 1):
                            pe.wait_ge(s_max, g * 16 + m - 1)
                        t, r = 2 * ((u + 2) % UNITS) + i // 2, (i % 2) * HALF
                        pe.matmul(max_ps[m % 2][:, :], q_rows[p][r:r + ROWS, t, qt * P:(qt + 1) * P],
                                  k_rows[p][r:r + ROWS, t, :], start=True, stop=True).then_inc(s_max_mm, 1)

                def scores(u, kt, i, slot):
                    if kt == 0 and i == 0:
                        pe.wait_ge(s_neg_rows, (b * UNITS + u + 1) * MAPS * DMA)
                    if finishes(k) and FFN_AT <= slot < FFN_AT + 3:
                        pe.wait_ge(s_gelu, (b - 1) * FC + (7, 8, 6)[slot - FFN_AT])
                    elif FFN_AT <= slot < FFN_AT + 3:
                        pe.wait_ge(s_exp, b * SLOTS + FFN_AT + (-1, 0, -2)[slot - FFN_AT])
                    else:
                        if due(b * SLOTS + slot - 2):
                            pe.wait_ge(s_exp, b * SLOTS + slot - 2)
                    t, r = 2 * u + SCORE_MAP[i] // 2, (SCORE_MAP[i] % 2) * HALF
                    pe.matmul(score_ps[score_bank(slot)][:, :], k_rows[par][r:r + HALF, t, kt * P:(kt + 1) * P],
                              q_rows[par][r:r + HALF, t, :], start=True, stop=True).then_inc(s_score_mm, 1)

                def value_sums(u, kt, batch, p):
                    n = batch * UNITS + u
                    if kt == 0:
                        if due(n):
                            pe.wait_ge(s_pair, n)
                        if u == 0:
                            pe.wait_ge(s_vals, (batch + 1) * 2)
                    pe.wait_ge(s_exp, (n * STEPS + kt + 1) * MAPS)
                    for i in range(MAPS):
                        last = pe.matmul(pv_ps[i * VW:(i + 1) * VW, :], vals[p][:, kt, 2 * u + i // 2, :],
                                         probs[:, kt % 2, i, :], start=(kt == 0), stop=(kt == STEPS - 1))
                    last.then_inc(s_pv_mm, 1)

                for slot in range(SLOTS):
                    u, kt, i = slot // 16, slot // 4 % 4, slot % 4
                    with_ffn, in_slots = maxima_at(k, u)
                    if slot == FFN_AT and finishes(k):
                        a = b - 1
                        pe.wait_ge(s_x2T, (a + 1) * 2)
                        for j in range(FC):
                            if j < 3:
                                pe.wait_ge(s_exp, b * SLOTS + (FFN_AT + (-1, 0, -2)[j] if attends(k) else 0))
                            else:
                                pe.wait_ge(s_gelu, a * FC + j - 2)
                            for c in range(EC):
                                for n in range(2):
                                    last = pe.matmul(score_ps[ffn_bank(j)][:, :], w1_tern[:, c, j * P:(j + 1) * P],
                                                     x2T[:, n, c, :], start=(c == 0 and n == 0), stop=(c == 1 and n == 1))
                            last.then_inc(s_ffn1_mm, 1)
                            maxima(u, with_ffn[j])
                    if k < 0 and slot == WTOT_PE:
                        pe.wait_ge(s_wsum, 2)
                        pe.matmul(y_ps[:, 0:2], ones, wsum[:, :], start=True, stop=True).then_inc(s_wtot, 1)
                    if k == 1 and slot == 0:
                        pe.wait_ge(s_const, CONST_LOADS * DMA)
                        pe.wait_ge(s_dve_set, DVE_SET)
                    if i >= 2:
                        maxima(u, in_slots[slot % 16])
                    if attends(k):
                        scores(u, kt, i, slot)
                    if i < 2:
                        maxima(u, in_slots[slot % 16])
                    if i == (2 if kt == 1 else 1):
                        if kt and attends(k):
                            value_sums(u, kt - 1, b, par)
                        elif not kt and u and attends(k):
                            value_sums(u - 1, STEPS - 1, b, par)
                        elif not kt and not u and attends(k - 1):
                            value_sums(UNITS - 1, STEPS - 1, b - 1, 1 - par)
                    if kt == 1 and i == 0 and has_head(k, u):
                        pe.wait_ge(s_pv_sb, b * UNITS + u)
                        for t in range(NT):
                            last = pe.transpose(pv_ps[:, t * P:(t + 1) * P], pv_sb[:, t * P:(t + 1) * P], ident[:, :])
                        last.then_inc(s_oT_mm, 1)
                    if slot % 16 == NEG_PE and has_neg(k, u):
                        if due(b * UNITS + u + 1):
                            pe.wait_ge(s_neg_sb, b * UNITS + u + 1)
                        if projects(k) and u == 1:
                            pe.wait_ge(s_xT, (b + 2) * 2)
                        if projects(k) and u in (2, 3):
                            pe.wait_ge(s_qk_whole, (b + 1) * 4 + 2 * (u - 1))
                        if projects(k) and (u == 4 or k < 0):
                            pe.wait_ge(s_vals, (b + 2) * 2)
                        pe.wait_ge(s_neg_parts, b * UNITS + u + 2)
                        for t in range(NT):
                            last = pe.transpose(neg_ps[0:3 * MAPS, t * P:(t + 1) * P],
                                                neg_parts[:, t * MAPS:(t + 1) * MAPS, :].rearrange("p i a -> p (i a)"), ident_b[:, :])
                        last.then_inc(s_neg_mm, 1)
                    if projects(k):
                        if slot in XT_PE:
                            c = XT_PE.index(slot)
                            if due(b * UNITS + 2):
                                pe.wait_ge(s_neg_sb, b * UNITS + 2)
                            if due((b + 1) * 2 + c):
                                pe.wait_ge(s_xT, (b + 1) * 2 + c)
                            pe.wait_ge(s_xn, b + 2)
                            for t in range(NT):
                                last = pe.transpose(x_ps[:, t * P:(t + 1) * P], xn[:, t, c * P:(c + 1) * P], ident[:, :])
                            last.then_inc(s_xT_mm, 1)
                        if slot in PROJ_PE:
                            n = PROJ_PE.index(slot)
                            if due(b * UNITS + 3 + n // 2):
                                pe.wait_ge(s_neg_sb, b * UNITS + 3 + n // 2)
                            if due((b + 1) * 4 + min(n, 4)):
                                pe.wait_ge(s_qk_whole, (b + 1) * 4 + min(n, 4))
                            if n == 5:
                                pe.wait_ge(s_vals, (b + 1) * 2 + 1)
                            if n == 0:
                                pe.wait_ge(s_xT, (b + 2) * 2)
                                if k < 0:
                                    pe.wait_ge(s_wqkv, DMA)
                            if n < 4:
                                for c in range(EC):
                                    last = pe.matmul(x_ps[:, :], wqkv_sb[:, c, n * P:(n + 1) * P], xnT[:, c, :],
                                                     start=(c == 0), stop=(c == 1))
                            else:
                                for t in range(2):
                                    at = (2 * (n - 4) + t) * P
                                    for c in range(EC):
                                        last = pe.matmul(x_ps[:, t * E:(t + 1) * E], xnT[:, c, at:at + P],
                                                         wqkv_sb[:, c, 2 * E:3 * E], start=(c == 0), stop=(c == 1))
                            last.then_inc(s_proj_mm, 1)
                    if finishes(k):
                        a = b - 1
                        if slot in WO_PE:
                            h = WO_PE.index(slot)
                            if due(a * 2):
                                pe.wait_ge(s_y, a * 2)
                            if due(a * NT + 2 * h):
                                pe.wait_ge(s_x2, a * NT + 2 * h)
                            pe.wait_ge(s_heads_n, (a + 1) * UNITS)
                            by_row = heads_n[:, :, :, :, :].rearrange("p c d h f -> p c (d h f)")
                            for t in range(2):
                                at = (2 * h + t) * P
                                for c in range(EC):
                                    last = pe.matmul(y_ps[:, t * E:(t + 1) * E], by_row[:, c, at:at + P], wo_sb[:, c, :],
                                                     start=(c == 0), stop=(c == 1))
                            last.then_inc(s_wo_mm, 1)
                        if slot in X2T_PE:
                            n = X2T_PE.index(slot)
                            pe.wait_ge(s_x2, (a + 1) * NT)
                            if due(a * 2 + n):
                                pe.wait_ge(s_x2T, a * 2 + n)
                            pe.wait_ge((s_x2_hi, s_x2_lo)[n], (2, 1)[n] * (a + 1))
                            for c in range(EC):
                                for t in range(NT):
                                    at = c * S + t * P
                                    last = pe.transpose(x2T_ps[:, at:at + P], x2hl[:, n, t, c * P:(c + 1) * P], ident_h[:, :])
                            last.then_inc(s_x2T_mm, 1)
                        if slot in FFN2_PE:
                            n = FFN2_PE.index(slot)
                            t, at = n // 4, (n // 4) % 2 * E
                            if n % 8 == 0:
                                pe.wait_ge(s_x2T, (a + 1) * 2)
                                if due(a * 2 + n // 8):
                                    pe.wait_ge(s_y, a * 2 + n // 8)
                                pe.wait_ge(s_h_lo, (a + 1) * FC)
                            for f in range(n % 4 * 2, n % 4 * 2 + 2):
                                for part in (h_hi, h_lo):
                                    last = pe.matmul(y_ps[:, at:at + E], part[:, f, t * P:(t + 1) * P], w2_tern[:, f, :],
                                                     start=(f == 0 and part is h_hi), stop=(f == FC - 1 and part is h_lo))
                            if n % 8 == 7:
                                last.then_inc(s_ffn2_mm, 1)

            frames(pe, frame)


_INS = ["x", "w_qkv", "wo", "lq1", "lq2", "lk1", "lk2", "norm_rows", "w1t", "b1c", "b1r", "w2t", "b2r"]


def kernel(L0_attn_x, L0_attn_w_qkv, L0_attn_wo, L0_attn_lambda_q1, L0_attn_lambda_q2, L0_attn_lambda_k1,
           L0_attn_lambda_k2, L0_attn_norm_w, L0_ffn_W1, L0_ffn_b1, L0_ffn_W2, L0_ffn_b2):
    import numpy as _np
    import concourse.bacc as _bacc
    from concourse import mybir as _mybir
    from concourse.bass_utils import run_bass_kernel_spmd as _run

    norm_w = _np.asarray(L0_attn_norm_w)
    by_row = _np.repeat(norm_w.T.reshape(-1), 2).reshape(NT, P).T
    laid = {
        "x": L0_attn_x, "w_qkv": L0_attn_w_qkv, "wo": L0_attn_wo,
        "lq1": L0_attn_lambda_q1, "lq2": L0_attn_lambda_q2, "lk1": L0_attn_lambda_k1, "lk2": L0_attn_lambda_k2,
        "norm_rows": by_row, "w1t": _np.asarray(L0_ffn_W1).T, "b1c": _np.asarray(L0_ffn_b1).reshape(FC, P).T,
        "b1r": L0_ffn_b1, "w2t": _np.asarray(L0_ffn_W2).T, "b2r": L0_ffn_b2,
    }
    nc = _bacc.Bacc("TRN2", target_bir_lowering=False, num_devices=1)
    arrays, args = {}, []
    for name in _INS:
        a = _np.ascontiguousarray(laid[name])
        arrays[f"in_{name}"] = a
        args.append(nc.dram_tensor(f"in_{name}", a.shape, _mybir.dt.from_np(a.dtype), kind="ExternalInput").ap())
    args.append(nc.dram_tensor("out", (B, S, E), F32, kind="ExternalOutput").ap())
    bass_diff_attention_ternary_ffn(nc, *args)
    r = _run(nc, [arrays], core_ids=[0])
    return r.results[0]["out"]
```

```python
import numpy as np
import concourse.bass as bass
from concourse import mybir
from contextlib import ExitStack

F32 = mybir.dt.float32
BF16 = mybir.dt.bfloat16
F16 = mybir.dt.float16
ALU = mybir.AluOpType
ACT = mybir.ActivationFunctionType
AX = mybir.AxisListType

P = 128
B, S, E, H = 32, 512, 256, 16
HD = E // H
QD = HD // 2
FF = 4 * E
NT = S // P
EC = E // P
FC = FF // P
UNITS, STEPS, MAPS = 8, 4, 4
SLOTS = UNITS * STEPS * MAPS
LAMBDA_INIT = 0.8
RMS_EPS = 1e-6
RMS_CHAIN = 7
LN_EPS = 1e-5
SCORE_SCALE = HD ** -0.5
VW = 32
HALF = 64
Q_PART = (0, 0, 0, 1, 1, 2)
K_PART = (0, 1, 2, 0, 1, 0)
ROWS = QD * len(Q_PART)
MROWS = ROWS + 3
DMA = 16
SCORE_MAP = (0, 2, 1, 3)
MAX_MAP = (1, 3, 0, 2)

STATS1_DVE, AGGR1_DVE, NORM1_DVE = ((74, 78, 83, 86), 87, (98, 103, 106, 110))
FIRST_STATS1_DVE, FIRST_AGGR1_DVE, FIRST_NORM1_DVE = (0, 1, 2, 3), 5, (8, 9, 10, 11)
XT_PE = (12, 18)
XT_ACT = (13, 18)
XHI_ACT, FIRST_XHI_ACT = (0, 3), (0, 1)
SUMS_PE = (1, 6, 9, 13)
PV_ACT, OT_PE = (1, 4)
PAIR_DVE, HEAD_DVE = (4, 9)
NEG_PE, NEG_ACT = (5, 6)
MAX_FIRST = (2, 3, 6, 7, 10, 11, 14, 15)
PROJ_PE = ((26, 28), (31, 33), (43, 44), (48, 49), (58, 59), (62, 63))
PROJ_ACT = (29, 34, 45, 50, 60, 65)
WO_PE = ((18, 19), (24, 25))
X2_DVE = ((21, 22), (25, 27))
STATS2_DVE = (24, 26, 29, 30)
AGGR2_DVE = 32
NORM2_DVE = (39, 42, 44, 45)
HI_ACT = (42, 46)
X2T_PE = (51, 55)
X2T_DVE = (52, 58)
FFN_UNIT = 4
LATE_TILES = (5, 6, 7)
H_HI_ACT, H_LO_DVE = ((71, 75, 79), (72, 78, 81))
FFN2_PE = [64, 65, 67, 68, 82, 86, 90, 94, 101, 103, 107, 110, 113, 116, 119, 122]
FFN2_ORDER = ((0, 0), (0, 1), (1, 0), (1, 1), (0, 2), (0, 3), (1, 2), (1, 3))
FFN2_ACT = (95, 126)
LAM_ACT, W_MAX_DVE, SETUP_DVE, WTOT_PE = 20, 7, 12, 50
DVE_SET, CONST_LOADS = 22, 9
TWO_ONES = float(np.array([0x3F803F80], np.uint32).view(np.float32)[0])
FFN_AT = FFN_UNIT * STEPS * MAPS


def score_bank(slot):
    return (slot if slot < FFN_AT else slot + 1) % 3


def ffn_bank(j):
    return (FFN_AT + 1 + j) % 3


def bass_diff_attention_ternary_ffn(nc, x_in, w_qkv, wo, lq1, lq2, lk1, lk2, norm_rows, w1t, b1c, b1r, w2t, b2r, out):
    scratch = nc.dram_tensor("qk_parts", [2, 2, 3, E, S], BF16, kind="Internal").ap()
    ctx = ExitStack()
    with ctx:
        def sb(name, shape, dt):
            return ctx.enter_context(nc.sbuf_tensor(name, shape, dt))

        def pb(name, shape, dt):
            return ctx.enter_context(nc.psum_tensor(name, shape, dt))

        def sem(name):
            return ctx.enter_context(nc.semaphore(name))

        q_rows = [sb(f"q_rows{p}", [P, H, S], BF16) for p in range(2)]
        k_rows = [sb(f"k_rows{p}", [P, H, S], BF16) for p in range(2)]
        vals = [sb(f"vals{p}", [P, NT, H, VW], F32) for p in range(2)]
        probs = sb("probs", [P, 2, MAPS, S], F32)
        wqkv_hl = sb("wqkv_hl", [P, 2, EC, 3 * E], F16)
        wo_sb = sb("wo_sb", [P, EC, E], F32)
        w1_tern = sb("w1_tern", [P, EC, FF], F16)
        w2_tern = sb("w2_tern", [P, FC, E], F16)
        x_sb = sb("x_sb", [P, NT, E], F32)
        xres = sb("xres", [P, NT, E], F32)
        xn = sb("xn", [P, NT, E], F32)
        xhl = sb("xhl", [P, 2, NT, E], F16)
        xT = sb("xT", [P, 2, EC, S], F16)
        parts = sb("parts", [P, 2, 3, S], BF16)
        qk_whole = sb("qk_whole", [P, 2, S], F32)
        y_sb = qk_whole
        pv_sb = sb("pv_sb", [P, S], F32)
        heads_n = sb("heads_n", [P, EC, HD, H, 2], F32)
        x2 = sb("x2", [P, NT, E], F32)
        x2b = sb("x2b", [P, NT, E], F32)
        x2n = sb("x2n", [P, NT, E], F32)
        x2hl = sb("x2hl", [P, 2, NT, E], F16)
        x2T = sb("x2T", [P, 2, EC, S], F16)
        hT = sb("hT", [P, FC, S], F32)
        h_hi = sb("h_hi", [P, FC, S], F16)
        h_lo = sb("h_lo", [P, FC, S], F16)
        ident = sb("ident", [P, P], F32)
        ident_b = sb("ident_b", [P, P], BF16)
        ident_h = sb("ident_h", [P, P], F16)
        b1_sb = sb("b1_sb", [P, FC], F32)
        b2_sb = sb("b2_sb", [P, E], F32)
        nw_raw = sb("nw_raw", [P, NT], F32)
        nw = sb("nw", [P, NT], F32)
        lam_in = sb("lam_in", [P, 4, QD * 2], F32)
        lam_pr = sb("lam_pr", [P, 2, QD * 2], F32)
        lam_dot = sb("lam_dot", [P, 2], F32)
        lam_exp = sb("lam_exp", [P, 2], F32)
        lam_neg = sb("lam_neg", [P, 1], F32)
        half_pow = sb("half_pow", [P, NT * 2], F32)
        zero = sb("zero", [P, 1], F32)
        ln_eps = sb("ln_eps", [P, NT], F32)
        rms_eps = sb("rms_eps", [P, NT * 2], F32)
        wsum = sb("wsum", [P, 2], F32)
        wthr = sb("wthr", [P, 2, 2], F32)
        w_max = sb("w_max", [P, 1], F32)
        tau = sb("tau", [P, 1], F32)
        tau_inv = sb("tau_inv", [P, 1], F32)
        h_bound = sb("h_bound", [P, 1], F32)
        sigma = sb("sigma", [P, 1], F32)
        sigma_inv = sb("sigma_inv", [P, 1], F32)
        st1 = sb("st1", [P, NT, 6], F32)
        mv1 = sb("mv1", [P, NT, 2], F32)
        ve1 = sb("ve1", [P, NT], F32)
        rstd1 = sb("rstd1", [P, NT], F32)
        st2 = sb("st2", [P, NT, 6], F32)
        mv2 = sb("mv2", [P, NT, 2], F32)
        ve2 = sb("ve2", [P, NT], F32)
        rstd2 = sb("rstd2", [P, NT], F32)
        neg = sb("neg", [P, 2, MAPS, NT], F32)
        neg_r = sb("neg_r", [P, MAPS, NT], F32)
        neg_cols = sb("neg_cols", [P, P], BF16)
        neg_parts = neg_cols[:, 0:MAPS * 3 * NT].rearrange("p (i a q) -> p i a q", i=MAPS, a=3)
        neg_rows = sb("neg_rows", [MAPS * 3 * NT, 2, P], BF16)
        den = sb("den", [P, NT * MAPS], F32)
        pair = sb("pair", [P, NT * MAPS, HD], F32)
        head = sb("head", [P, NT * 2, HD], F32)
        head_sq = sb("head_sq", [P, NT * 2, HD], F32)
        ms = sb("ms", [P, NT * 2], F32)
        rrms = sb("rrms", [P, NT * 2], F32)
        w1_raw = probs[:, 0, :, :].rearrange("p a s -> p (a s)").rearrange("p (c f) -> p c f", c=EC)
        w2_raw = probs[:, 1, :, :].rearrange("p a s -> p (a s)").rearrange("p (c f) -> p c f", c=FC)
        ones = hT[:, 4, 0:P]
        wqkv_raw = hT[:, 5:8, :].rearrange("p a s -> p (a s)").rearrange("p (c n) -> p c n", c=EC)
        w_below = hT[:, 0:4, :].rearrange("p a s -> p (a s)")

        score_ps = [pb(f"score_ps{i}", [P, S], F32) for i in range(3)]
        max_ps = [pb(f"max_ps{i}", [P, S], F32) for i in range(2)]
        pv_ps = pb("pv_ps", [P, S], F32)
        x_ps = pb("x_ps", [P, S], F32)
        y_ps = pb("y_ps", [P, S], F32)
        neg_ps = x_ps[:, :].bitcast(BF16)
        xT_ps = x_ps[:, :].bitcast(F16)
        x2T_ps = y_ps[:, :].bitcast(F16)

        s_const = sem("s_const")
        s_wqkv = sem("s_wqkv")
        s_w = sem("s_w")
        s_x = sem("s_x")
        s_xres = sem("s_xres")
        s_parts_out = [sem("s_parts_out0"), sem("s_parts_out1")]
        s_q_rows = sem("s_q_rows")
        s_k_rows = sem("s_k_rows")
        s_neg_rows = sem("s_neg_rows")
        s_out = sem("s_out")
        s_pool_set = sem("s_pool_set")
        s_dve_set = sem("s_dve_set")
        s_rows_set = sem("s_rows_set")
        s_lam_dot = sem("s_lam_dot")
        s_lam_exp = sem("s_lam_exp")
        s_w_max = sem("s_w_max")
        s_w_bound = sem("s_w_bound")
        s_wqkv_hl = sem("s_wqkv_hl")
        s_wsum = sem("s_wsum")
        s_wtot = sem("s_wtot")
        s_xT_mm = sem("s_xT_mm")
        s_proj_mm = sem("s_proj_mm")
        s_max_mm = sem("s_max_mm")
        s_neg_mm = sem("s_neg_mm")
        s_score_mm = sem("s_score_mm")
        s_pv_mm = sem("s_pv_mm")
        s_oT_mm = sem("s_oT_mm")
        s_wo_mm = sem("s_wo_mm")
        s_x2T_mm = sem("s_x2T_mm")
        s_ffn1_mm = sem("s_ffn1_mm")
        s_ffn2_mm = sem("s_ffn2_mm")
        s_x_hi = sem("s_x_hi")
        s_xT = sem("s_xT")
        s_h_part = sem("s_h_part")
        s_qk_whole = sem("s_qk_whole")
        s_vals = sem("s_vals")
        s_exp = sem("s_exp")
        s_pv_sb = sem("s_pv_sb")
        s_gelu = sem("s_gelu")
        s_h_hi = sem("s_h_hi")
        s_x2_hi = sem("s_x2_hi")
        s_y = sem("s_y")
        s_st1 = sem("s_st1")
        s_mv1 = sem("s_mv1")
        s_xn = sem("s_xn")
        s_max = sem("s_max")
        s_neg_sb = sem("s_neg_sb")
        s_den = sem("s_den")
        s_pair = sem("s_pair")
        s_head = sem("s_head")
        s_x2 = sem("s_x2")
        s_st2 = sem("s_st2")
        s_mv2 = sem("s_mv2")
        s_x2n = sem("s_x2n")
        s_x2T = sem("s_x2T")
        s_h_lo = sem("s_h_lo")
        s_rstd1 = sem("s_rstd1")
        s_rest = sem("s_rest")
        s_mid = sem("s_mid")
        s_parts = sem("s_parts")
        s_neg_chain = sem("s_neg_chain")
        s_neg_parts = sem("s_neg_parts")
        s_rms_chain = sem("s_rms_chain")
        s_heads_n = sem("s_heads_n")
        s_rstd2 = sem("s_rstd2")
        s_x_lo = sem("s_x_lo")
        s_ve1 = sem("s_ve1")
        s_ve2 = sem("s_ve2")
        s_x2_lo = sem("s_x2_lo")
        s_x2b = sem("s_x2b")
        s_out_sum = sem("s_out_sum")

        def due(count):
            return not isinstance(count, int) or count > 0

        def frames(eng, frame):
            for b in (-1, 0, 1):
                frame(b, b, b % 2)
            with eng.Fori(0, (B - 4) // 2) as i:
                frame(i * 2 + 2, 2, 0)
                frame(i * 2 + 3, 3, 1)
            for b in (B - 2, B - 1, B):
                frame(b, b, b % 2)

        def projects(k):
            return k + 1 < B

        def attends(k):
            return 0 <= k < B

        def finishes(k):
            return k >= 1

        def has_max(k, u):
            return 0 <= k * UNITS + u + 2 < B * UNITS

        def has_neg(k, u):
            return 0 <= k * UNITS + u + 1 < B * UNITS

        def has_head(k, u):
            return 0 <= k * UNITS + u - 1 < B * UNITS

        def maxima_at(k, u):
            if not has_max(k, u):
                return [()] * FC, [()] * 16
            if u == FFN_UNIT and finishes(k):
                return [(j,) for j in range(FC)], [(8 + n // 2,) if n % 2 else () for n in range(16)]
            return [()] * FC, [(n,) for n in range(16)]

        block = ctx.enter_context(nc.Block())

        @block.sync
        def _(sp):
            sp.dma_start(x_sb[:, :, :], x_in[0].rearrange("(t p) e -> p t e", p=P)).then_inc(s_x, DMA)
            sp.dma_start(wqkv_raw, w_qkv.rearrange("(c p) n -> p c n", p=P)).then_inc(s_wqkv, DMA)
            for n, v in enumerate((lq1, lk1, lq2, lk2)):
                sp.dma_start(lam_in[:, n, :], v.partition_broadcast(P)).then_inc(s_const, DMA)
            sp.dma_start(nw_raw[:, :], norm_rows).then_inc(s_const, DMA)
            sp.dma_start(x2b[:, :, :].rearrange("p t e -> p (t e)"), b1r.partition_broadcast(P)).then_inc(s_const, DMA)
            sp.dma_start(b1_sb[:, :], b1c).then_inc(s_const, DMA)
            sp.dma_start(b2_sb[:, :], b2r.partition_broadcast(P)).then_inc(s_const, DMA)
            sp.dma_start(wo_sb[:, :, :], wo.rearrange("(c p) n -> p c n", p=P)).then_inc(s_const, DMA)
            sp.dma_start(w1_raw, w1t.rearrange("(c p) f -> p c f", p=P)).then_inc(s_w, DMA)
            sp.dma_start(w2_raw, w2t.rearrange("(c p) f -> p c f", p=P)).then_inc(s_w, DMA)

            def frame(b, k, par):
                for u in range(UNITS):
                    if u == 1 and k + 2 < B:
                        sp.wait_ge(s_xn, b + 2)
                        sp.dma_start(x_sb[:, :, :], x_in[b + 2].rearrange("(t p) e -> p t e", p=P)).then_inc(s_x, DMA)
                    if has_neg(k, u):
                        g = (u + 1) % UNITS
                        n = b * UNITS + u + 1
                        sp.wait_ge(s_neg_sb, n + 1)
                        dst = q_rows[par if u + 1 < UNITS else 1 - par]
                        for i in range(MAPS):
                            at = (i % 2) * HALF + ROWS
                            sp.dma_start(dst[at:at + 3, 2 * g + i // 2, :],
                                         neg_rows[3 * NT * i:3 * NT * (i + 1), (u + 1) % 2, :])\
                              .then_inc(s_neg_rows, DMA)
                    if projects(k):
                        qk = {2: 0, 4: 1}.get(u)
                        if qk is not None:
                            for ft in range(EC):
                                n = 2 * qk + ft
                                sp.wait_ge(s_h_part, (b + 1) * 4 + n + 1)
                                sp.wait_ge(s_parts, (b + 1) * 4 + n + 1)
                                sp.dma_start(scratch[1 - par, qk, :, ft * P:(ft + 1) * P, :].rearrange("a f s -> f a s"),
                                             parts[:, n % 2, :, :]).then_inc(s_parts_out[n % 2], DMA)
                            for n in range(2):
                                sp.wait_ge(s_parts_out[n], ((b + 1) * 2 + qk + 1) * DMA)
                            dst, order, done = ((q_rows[1 - par], Q_PART, s_q_rows), (k_rows[1 - par], K_PART, s_k_rows))[qk]
                            if k <= 0:
                                sp.wait_ge(s_rows_set, 2 * (k + 2))
                            for r in range(2):
                                for row, part in enumerate(order):
                                    src = scratch[1 - par, qk, part, :, :].rearrange("(t r d) s -> r d t s", r=2, d=QD)
                                    at = r * HALF + row * QD
                                    sp.dma_start(dst[at:at + QD, :, :], src[r]).then_inc(done, DMA)
                    if u == 3 and attends(k):
                        if due(b * NT):
                            sp.wait_ge(s_x2, b * NT)
                        sp.dma_start(xres[:, :, :], x_in[b].rearrange("(t p) e -> p t e", p=P)).then_inc(s_xres, DMA)
                    if u == 7 and finishes(k):
                        sp.wait_ge(s_out_sum, (b - 1) * 2 + 1)
                        sp.dma_start(out[b - 1, 0:2 * P, :].rearrange("(t p) e -> p t e", p=P), x2b[:, 0:2, :]).then_inc(s_out, DMA)
                    if u == 7 and finishes(k):
                        sp.wait_ge(s_out_sum, (b - 1) * 2 + 2)
                        sp.dma_start(out[b - 1, 2 * P:4 * P, :].rearrange("(t p) e -> p t e", p=P), x2b[:, 2:4, :]).then_inc(s_out, DMA)

            frames(sp, frame)
            sp.wait_ge(s_out, B * 2 * DMA)

        @block.gpsimd
        def _(pool):
            for m in (ident, ident_b, ident_h):
                pool.memset(m[:, :], 0.0)
            pool.memset(ones, 1.0)
            pool.memset(half_pow[:, :], -0.5)
            pool.memset(zero[:, :], 0.0)
            pool.memset(ln_eps[:, :], LN_EPS)
            pool.memset(rms_eps[:, :], HD * RMS_EPS)
            pool.memset(neg_cols[:, :], 0.0).then_inc(s_pool_set, 1)
            pool.wait_ge(s_pool_set, 1)
            for m in (ident, ident_b, ident_h):
                last = pool.affine_select(out=m[:, :], in_=m[:, :], compare_op=ALU.not_equal, fill=1.0,
                                          base=0, pattern=[[-1, P]], channel_multiplier=1)
            last.then_inc(s_pool_set, 1)

            def rstd(mv, ve, r, moments_ready, ve_ready, rstd_ready, n):
                pool.wait_ge(moments_ready, n + 1)
                pool.tensor_tensor(ve[:, :], mv[:, :, 1], ln_eps[:, :], ALU.add).then_inc(ve_ready, 1)
                pool.wait_ge(ve_ready, n + 1)
                pool.tensor_tensor(r[:, :], ve[:, :], half_pow[:, 0:NT], ALU.pow).then_inc(rstd_ready, 1)

            def split(b, n):
                c = (b + 1) * 4 + n
                pool.wait_ge(s_h_part, c + 1)
                pool.wait_ge(s_qk_whole, c + 1)
                pool.tensor_tensor(qk_whole[:, n % 2, :], qk_whole[:, n % 2, :], parts[:, n % 2, 0, :], ALU.subtract).then_inc(s_rest, 1)
                pool.wait_ge(s_rest, c + 1)
                pool.tensor_tensor(parts[:, n % 2, 1, :], qk_whole[:, n % 2, :], zero[:, :].broadcast_to([P, S]), ALU.add).then_inc(s_mid, 1)
                pool.wait_ge(s_mid, c + 1)
                pool.tensor_tensor(parts[:, n % 2, 2, :], qk_whole[:, n % 2, :], parts[:, n % 2, 1, :], ALU.subtract).then_inc(s_parts, 1)

            def add_y(a, n):
                pool.wait_ge(s_x2b, a + 1)
                pool.wait_ge(s_y, a * 2 + n + 1)
                half = x2b[:, 2 * n:2 * n + 2, :].rearrange("p t e -> p (t e)")
                pool.tensor_tensor(half, y_sb[:, n, :], half, ALU.add).then_inc(s_out_sum, 1)

            def frame(b, k, par):
                for u in range(UNITS):
                    if u == 0 and k < 0:
                        rstd(mv1, ve1, rstd1, s_mv1, s_ve1, s_rstd1, 0)
                    if u == 0 and projects(k):
                        pool.wait_ge(s_xn, b + 2)
                        pool.wait_ge(s_x_hi, (b + 2) * 2)
                        if due((b + 1) * 2):
                            pool.wait_ge(s_xT_mm, (b + 1) * 2)
                        pool.tensor_tensor(xhl[:, 1, :, :], xn[:, :, :], xhl[:, 0, :, :], ALU.subtract).then_inc(s_x_lo, 1)
                    if u == 0 and k < 0:
                        for p in range(2):
                            last = pool.memset(vals[p][:, :, :, :], 0.0)
                        last.then_inc(s_pool_set, 1)
                        pool.wait_ge(s_pool_set, 3)
                        for p in range(2):
                            last = pool.memset(vals[p][:, :, :, HD:HD + 1], 1.0)
                        last.then_inc(s_pool_set, 1)
                    if u == 6 and k + 2 < B:
                        rstd(mv1, ve1, rstd1, s_mv1, s_ve1, s_rstd1, b + 2)
                    if u == 3 and finishes(k):
                        pool.wait_ge(s_x2n, b * NT)
                        pool.wait_ge(s_x2_hi, b * 2)
                        if due((b - 1) * 2):
                            pool.wait_ge(s_x2T_mm, (b - 1) * 2)
                        pool.tensor_tensor(x2hl[:, 1, :, :], x2n[:, :, :], x2hl[:, 0, :, :], ALU.subtract).then_inc(s_x2_lo, 1)
                    if projects(k) and u in (2, 3):
                        split(b, u - 1)
                    if u == 5 and finishes(k):
                        if due((b - 1) * 2 * DMA):
                            pool.wait_ge(s_out, (b - 1) * 2 * DMA)
                        pool.wait_ge(s_x2, b * NT)
                        if k == 1:
                            pool.wait_ge(s_const, CONST_LOADS * DMA)
                        pool.tensor_tensor(x2b[:, :, :], x2[:, :, :],
                                           b2_sb[:, :].unsqueeze(1).broadcast_to([P, NT, E]), ALU.add).then_inc(s_x2b, 1)
                    if has_head(k, u):
                        n = b * UNITS + u - 1
                        g = (u - 1) % UNITS
                        pool.wait_ge(s_head, n + 1)
                        pool.tensor_tensor(head_sq[:, :, :], head[:, :, :], head[:, :, :], ALU.mult).then_inc(s_rms_chain, 1)
                        for f, w in enumerate((HD // 2, HD // 4, HD // 8, 1)):
                            pool.wait_ge(s_rms_chain, RMS_CHAIN * n + f + 1)
                            pool.tensor_tensor(head_sq[:, :, 0:w], head_sq[:, :, 0:w], head_sq[:, :, w:2 * w], ALU.add)\
                                .then_inc(s_rms_chain, 1)
                        pool.wait_ge(s_rms_chain, RMS_CHAIN * n + 5)
                        pool.tensor_tensor(ms[:, :], head_sq[:, :, 0], rms_eps[:, :], ALU.add).then_inc(s_rms_chain, 1)
                        pool.wait_ge(s_rms_chain, RMS_CHAIN * n + 6)
                        pool.tensor_tensor(rrms[:, :], ms[:, :], half_pow[:, 0:NT * 2], ALU.pow).then_inc(s_rms_chain, 1)
                        pool.wait_ge(s_rms_chain, RMS_CHAIN * (n + 1))
                        if g == 0:
                            if due((b if u else b - 1) * 2):
                                pool.wait_ge(s_wo_mm, (b if u else b - 1) * 2)
                        for f in range(2):
                            last = pool.tensor_tensor(
                                heads_n[:, :, :, 2 * g:2 * g + 2, f].rearrange("p c d h -> p c h d"),
                                head[:, f * 4:f * 4 + 4, :].rearrange("p (c h) d -> p c h d", h=2),
                                rrms[:, f * 4:f * 4 + 4].rearrange("p (c h) -> p c h", h=2).unsqueeze(3).broadcast_to([P, EC, 2, HD]),
                                ALU.mult)
                        last.then_inc(s_heads_n, 1)
                    if projects(k) and u in (1, 3):
                        split(b, 0 if u == 1 else 3)
                    if u == 1 and finishes(k):
                        rstd(mv2, ve2, rstd2, s_mv2, s_ve2, s_rstd2, b - 1)
                    if u == 6 and finishes(k):
                        add_y(b - 1, 0)
                    if has_max(k, u):
                        n = b * UNITS + u + 2
                        pool.wait_ge(s_max, 16 * (n + 1))
                        if due(n):
                            pool.wait_ge(s_neg_mm, n)
                        src = neg[:, u % 2, :, :]
                        pool.tensor_tensor(neg_parts[:, :, 0, :], src, zero[:, :].unsqueeze(2).broadcast_to([P, MAPS, NT]), ALU.add).then_inc(s_neg_chain, 1)
                        pool.wait_ge(s_neg_chain, 3 * n + 1)
                        pool.tensor_tensor(neg_r[:, :, :], src, neg_parts[:, :, 0, :], ALU.subtract).then_inc(s_neg_chain, 1)
                        pool.wait_ge(s_neg_chain, 3 * n + 2)
                        pool.tensor_tensor(neg_parts[:, :, 1, :], neg_r[:, :, :], zero[:, :].unsqueeze(2).broadcast_to([P, MAPS, NT]), ALU.add).then_inc(s_neg_chain, 1)
                        pool.wait_ge(s_neg_chain, 3 * n + 3)
                        pool.tensor_tensor(neg_parts[:, :, 2, :], neg_r[:, :, :], neg_parts[:, :, 1, :], ALU.subtract).then_inc(s_neg_parts, 1)
                    if u == 7 and finishes(k):
                        add_y(b - 1, 1)

            frames(pool, frame)

        @block.scalar
        def _(act):
            def high_half(a, j):
                act.wait_ge(s_gelu, a * FC + j + 1)
                act.activation(h_hi[:, j, :], hT[:, j, :], ACT.Copy, scale=sigma[:, 0:1]).then_inc(s_h_hi, 1)

            def frame(b, k, par):
                for slot in range(SLOTS):
                    u, kt, i = slot // 16, slot // 4 % 4, slot % 4
                    if k < 0 and slot == LAM_ACT:
                        act.wait_ge(s_lam_dot, 2)
                        act.activation(lam_exp[:, :], lam_dot[:, :], ACT.Exp).then_inc(s_lam_exp, 1)
                    if slot == FFN_AT and finishes(k):
                        if k == 1:
                            act.wait_ge(s_const, CONST_LOADS * DMA)
                        for j in range(FC):
                            act.wait_ge(s_ffn1_mm, (b - 1) * FC + j + 1)
                            if j == 0:
                                if due((b - 1) * 2):
                                    act.wait_ge(s_ffn2_mm, (b - 1) * 2)
                            act.activation(hT[:, j, :], score_ps[ffn_bank(j)][:, :], ACT.Gelu,
                                           bias=b1_sb[:, j:j + 1]).then_inc(s_gelu, 1)
                            if 0 < j <= LATE_TILES[0]:
                                high_half(b - 1, j - 1)
                    if attends(k):
                        act.wait_ge(s_score_mm, b * SLOTS + slot + 1)
                        if i == 0:
                            if due((b * UNITS + u) * STEPS + kt - 1):
                                act.wait_ge(s_pv_mm, (b * UNITS + u) * STEPS + kt - 1)
                        act.activation(probs[:, kt % 2, SCORE_MAP[i], :], score_ps[score_bank(slot)][:, :], ACT.Exp,
                                       scale=SCORE_SCALE).then_inc(s_exp, 1)
                    if slot % 16 == PV_ACT and has_head(k, u):
                        n = b * UNITS + u - 1
                        act.wait_ge(s_pv_mm, (n + 1) * STEPS)
                        if due(n):
                            act.wait_ge(s_oT_mm, n)
                        act.activation(pv_sb[:, :], pv_ps[:, :], ACT.Copy).then_inc(s_pv_sb, 1)
                    if slot % 16 == NEG_ACT and has_neg(k, u):
                        n = b * UNITS + u + 1
                        act.wait_ge(s_neg_mm, n + 1)
                        if due((n - 1) * MAPS * DMA):
                            act.wait_ge(s_neg_rows, (n - 1) * MAPS * DMA)
                        act.activation(neg_rows[:, (u + 1) % 2, :], neg_ps[0:MAPS * 3 * NT, 0:P], ACT.Copy).then_inc(s_neg_sb, 1)
                    if projects(k):
                        if slot in (XHI_ACT if k >= 0 else FIRST_XHI_ACT):
                            h = (XHI_ACT if k >= 0 else FIRST_XHI_ACT).index(slot)
                            act.wait_ge(s_xn, b + 2)
                            if due((b + 1) * 2):
                                act.wait_ge(s_xT_mm, (b + 1) * 2)
                            if due(b + 1):
                                act.wait_ge(s_x_lo, b + 1)
                            act.activation(xhl[:, 0, 2 * h:2 * h + 2, :], xn[:, 2 * h:2 * h + 2, :], ACT.Copy).then_inc(s_x_hi, 1)
                        if slot in XT_ACT:
                            c = XT_ACT.index(slot)
                            act.wait_ge(s_xT_mm, (b + 1) * 2 + c + 1)
                            if due((b + 1) * 6):
                                act.wait_ge(s_proj_mm, (b + 1) * 6)
                            act.activation(xT[:, c, :, :].rearrange("p c s -> p (c s)"), xT_ps, ACT.Copy).then_inc(s_xT, 1)
                        if slot in PROJ_ACT:
                            n = PROJ_ACT.index(slot)
                            act.wait_ge(s_proj_mm, (b + 1) * 6 + n + 1)
                            if n < 4:
                                if due(((b + 1) * 2 + n // 2) * DMA):
                                    act.wait_ge(s_parts_out[n % 2], ((b + 1) * 2 + n // 2) * DMA)
                                act.activation(parts[:, n % 2, 0, :], x_ps[:, :], ACT.Copy, scale=tau_inv[:, 0:1]).then_inc(s_h_part, 1)
                                if due((b - 1) * 2):
                                    act.wait_ge(s_out_sum, (b - 1) * 2)
                                if due((b + 1) * 4 + n - 1):
                                    act.wait_ge(s_parts, (b + 1) * 4 + n - 1)
                                act.activation(qk_whole[:, n % 2, :], x_ps[:, :], ACT.Copy, scale=tau_inv[:, 0:1]).then_inc(s_qk_whole, 1)
                            else:
                                t = 2 * (n - 4)
                                if k < 0:
                                    act.wait_ge(s_pool_set, 4)
                                act.activation(vals[1 - par][:, t:t + 2, :, 0:HD].rearrange("p t h d -> p (t h) d"),
                                               x_ps[:, :].rearrange("p (t d) -> p t d", d=HD), ACT.Copy, scale=tau_inv[:, 0:1])\
                                   .then_inc(s_vals, 1)
                    if slot in H_HI_ACT and finishes(k):
                        high_half(b - 1, LATE_TILES[H_HI_ACT.index(slot)])
                    if slot in FFN2_ACT and finishes(k):
                        h = FFN2_ACT.index(slot)
                        act.wait_ge(s_ffn2_mm, (b - 1) * 2 + h + 1)
                        if projects(k):
                            act.wait_ge(s_parts, (b + 2) * 4)
                        act.activation(y_sb[:, h, :], y_ps[:, :], ACT.Copy, scale=sigma_inv[:, 0:1]).then_inc(s_y, 1)
                    if slot in HI_ACT and finishes(k):
                        h = HI_ACT.index(slot)
                        act.wait_ge(s_x2n, (b - 1) * NT + 2 * h + 2)
                        if due((b - 1) * 2):
                            act.wait_ge(s_x2T_mm, (b - 1) * 2)
                        if due(b - 1):
                            act.wait_ge(s_x2_lo, b - 1)
                        act.activation(x2hl[:, 0, 2 * h:2 * h + 2, :], x2n[:, 2 * h:2 * h + 2, :], ACT.Copy).then_inc(s_x2_hi, 1)

            frames(act, frame)

        @block.vector
        def _(dve):
            steps = [0]

            def link(ins):
                steps[0] += 1
                ins.then_inc(s_dve_set, 1)
                dve.wait_ge(s_dve_set, steps[0])

            def split_wqkv():
                dve.wait_ge(s_w_bound, 1)
                link(dve.tensor_scalar(w_max[:, :], y_ps[:, 4:5], 1e-30, None, ALU.max))
                link(dve.tensor_scalar(w_max[:, :].bitcast(mybir.dt.uint32), w_max[:, :].bitcast(mybir.dt.uint32), 0x7F800000, None,
                                       ALU.bitwise_and))
                link(dve.tensor_scalar(tau_inv[:, :], w_max[:, :], 2.0 ** -13, None, ALU.mult))
                link(dve.reciprocal(tau[:, :], tau_inv[:, :]))
                link(dve.tensor_scalar(wqkv_hl[:, 0, :, :], wqkv_raw, tau[:, 0:1], None, ALU.mult))
                dve.scalar_tensor_tensor(wqkv_hl[:, 1, :, :], wqkv_raw, tau[:, 0:1], wqkv_hl[:, 0, :, :],
                                         ALU.mult, ALU.subtract).then_inc(s_wqkv_hl, 1)

            def set_up():
                dve.wait_ge(s_const, CONST_LOADS * DMA)
                link(dve.tensor_tensor(lam_pr[:, :, :], lam_in[:, 0:4:2, :], lam_in[:, 1:4:2, :], ALU.mult))
                dve.tensor_reduce(lam_dot[:, :], lam_pr[:, :, :], AX.X, ALU.add).then_inc(s_lam_dot, 2)
                link(dve.tensor_scalar(nw[:, :], nw_raw[:, :], (1.0 - LAMBDA_INIT) * HD ** 0.5, None, ALU.mult))
                for p in range(2):
                    for rows, value in ((q_rows[p], 0.0), (k_rows[p], TWO_ONES)):
                        dve.memset(rows[:, :, :].rearrange("p t s -> p (t s)").bitcast(F32), value).then_inc(s_rows_set, 1)
                dve.wait_ge(s_lam_exp, 1)
                link(dve.tensor_tensor(lam_neg[:, :], lam_exp[:, 0:1], lam_exp[:, 1:2], ALU.subtract))
                link(dve.tensor_scalar(lam_neg[:, :], lam_neg[:, :], -1.0, -LAMBDA_INIT, ALU.mult, ALU.add))
                link(dve.tensor_reduce(h_bound[:, :], x2b[:, :, :], AX.XY, ALU.max, apply_absolute_value=True))
                link(dve.tensor_scalar(h_bound[:, :], h_bound[:, :], float(E), None, ALU.add))
                link(dve.tensor_scalar(h_bound[:, :].bitcast(mybir.dt.uint32), h_bound[:, :].bitcast(mybir.dt.uint32), 0x7F800000, None,
                                       ALU.bitwise_and))
                link(dve.tensor_scalar(sigma_inv[:, :], h_bound[:, :], 2.0 ** -14, None, ALU.mult))
                link(dve.reciprocal(sigma[:, :], sigma_inv[:, :]))
                dve.wait_ge(s_w, 2 * DMA)
                for n, raw in enumerate((w1_raw, w2_raw)):
                    dve.tensor_reduce(wsum[:, n:n + 1], raw, AX.XY, ALU.add, apply_absolute_value=True).then_inc(s_wsum, 1)
                dve.wait_ge(s_wtot, 1)
                for n in range(2):
                    link(dve.tensor_scalar(wthr[:, 0, n:n + 1], y_ps[:, n:n + 1], 1.0 / (FF * E), 1e-8, ALU.mult, ALU.max))
                link(dve.tensor_scalar(wthr[:, 1, :], wthr[:, 0, :], -0.5, None, ALU.mult))
                link(dve.tensor_scalar(wthr[:, 0, :], wthr[:, 0, :], 0.5, None, ALU.mult))
                for n, (raw, tern) in enumerate(((w1_raw, w1_tern), (w2_raw, w2_tern))):
                    a, b = raw.rearrange("p c f -> p (c f)"), tern[:, :, :].rearrange("p c f -> p (c f)")
                    link(dve.tensor_scalar(w_below, a, wthr[:, 1, n:n + 1], None, ALU.is_lt))
                    link(dve.scalar_tensor_tensor(b, a, wthr[:, 0, n:n + 1], w_below, ALU.is_gt, ALU.subtract))
                assert steps[0] == DVE_SET

            def frame(b, k, par):
                def maxima(u, which):
                    g = b * UNITS + u + 2
                    for m in which:
                        dve.wait_ge(s_max_mm, g * 16 + m + 1)
                        if m == 0:
                            if due(g - 1):
                                dve.wait_ge(s_neg_parts, g - 1)
                        qt, i = m // 4, MAX_MAP[m % 4]
                        dve.tensor_reduce(neg[:, u % 2, i, qt:qt + 1], max_ps[m % 2][:, :], AX.X, ALU.max, negate=True)\
                           .then_inc(s_max, 1)

                def low_half(a, j):
                    dve.wait_ge(s_h_hi, a * FC + j + 1)
                    if j == 0 and due(a * 2):
                        dve.wait_ge(s_ffn2_mm, a * 2)
                    dve.scalar_tensor_tensor(h_lo[:, j, :], hT[:, j, :], sigma[:, 0:1], h_hi[:, j, :],
                                             ALU.mult, ALU.subtract).then_inc(s_h_lo, 1)

                def layernorm1(a, slot, stats_at, aggr_at, norm_at):
                    if slot in stats_at:
                        t = stats_at.index(slot)
                        dve.wait_ge(s_x, (a + 1) * DMA)
                        dve.bn_stats(st1[:, t, :], x_sb[:, t, :]).then_inc(s_st1, 1)
                    if slot == aggr_at:
                        if k < 0:
                            dve.wait_ge(s_st1, (a + 1) * NT)
                        for t in range(NT):
                            last = dve.bn_aggr(mv1[:, t, :], st1[:, t, :])
                        last.then_inc(s_mv1, 1)
                    if slot in norm_at:
                        dve.wait_ge(s_rstd1, a + 1)
                        if due(a):
                            dve.wait_ge(s_x_lo, a)
                        t = norm_at.index(slot)
                        last = dve.tensor_scalar(xn[:, t, :], x_sb[:, t, :], mv1[:, t, 0:1], rstd1[:, t:t + 1], ALU.subtract, ALU.mult)
                        if t == NT - 1:
                            last.then_inc(s_xn, 1)

                for slot in range(SLOTS):
                    u, kt, i = slot // 16, slot // 4 % 4, slot % 4
                    with_ffn, in_slots = maxima_at(k, u)
                    if slot == FFN_AT and finishes(k):
                        for j in range(FC):
                            maxima(u, with_ffn[j])
                            if 2 <= j < LATE_TILES[0] + 2:
                                low_half(b - 1, j - 2)
                    if slot == AGGR1_DVE and k + 2 < B:
                        dve.wait_ge(s_st1, (b + 3) * NT)
                    if slot == AGGR2_DVE and finishes(k):
                        dve.wait_ge(s_st2, b * NT)
                    maxima(u, in_slots[slot % 16])
                    if slot % 16 == PAIR_DVE and has_head(k, u):
                        n = b * UNITS + u - 1
                        sums = pv_ps[:, :].rearrange("p (n w) -> p n w", w=VW)
                        dve.wait_ge(s_oT_mm, n + 1)
                        dve.reciprocal(den[:, :], sums[:, :, HD]).then_inc(s_den, 1)
                        dve.wait_ge(s_den, n + 1)
                        dve.tensor_tensor(pair[:, :, :], sums[:, :, 0:HD],
                                          den[:, :].unsqueeze(2).broadcast_to([P, NT * MAPS, HD]), ALU.mult).then_inc(s_pair, 1)
                    if slot % 16 == HEAD_DVE and has_head(k, u):
                        n = b * UNITS + u - 1
                        dve.wait_ge(s_pair, n + 1)
                        if due(n):
                            dve.wait_ge(s_heads_n, n)
                        two = pair[:, :, :].rearrange("p (n j) d -> p n j d", j=2)
                        dve.scalar_tensor_tensor(head[:, :, :], two[:, :, 1, :], lam_neg[:, 0:1], two[:, :, 0, :],
                                                 ALU.mult, ALU.add).then_inc(s_head, 1)
                    if k < 0:
                        layernorm1(0, slot, FIRST_STATS1_DVE, FIRST_AGGR1_DVE, FIRST_NORM1_DVE)
                        if slot == W_MAX_DVE:
                            dve.wait_ge(s_wqkv, DMA)
                            dve.tensor_reduce(w_max[:, :], wqkv_raw, AX.XY, ALU.max, apply_absolute_value=True).then_inc(s_w_max, 1)
                        if slot == SETUP_DVE:
                            split_wqkv()
                            set_up()
                    if k + 2 < B:
                        layernorm1(b + 2, slot, STATS1_DVE, AGGR1_DVE, NORM1_DVE)
                    if finishes(k):
                        a = b - 1
                        for h in range(2):
                            if slot in X2_DVE[h]:
                                t = 2 * h + X2_DVE[h].index(slot)
                                dve.wait_ge(s_wo_mm, a * 2 + h + 1)
                                dve.wait_ge(s_xres, (a + 1) * DMA)
                                if due(a):
                                    dve.wait_ge(s_x2b, a)
                                dve.scalar_tensor_tensor(x2[:, t, :], y_ps[:, (t % 2) * E:(t % 2 + 1) * E], nw[:, t:t + 1],
                                                         xres[:, t, :], ALU.mult, ALU.add).then_inc(s_x2, 1)
                        if slot in STATS2_DVE:
                            t = STATS2_DVE.index(slot)
                            dve.wait_ge(s_x2, a * NT + t + 1)
                            dve.bn_stats(st2[:, t, :], x2[:, t, :]).then_inc(s_st2, 1)
                        if slot == AGGR2_DVE:
                            for t in range(NT):
                                last = dve.bn_aggr(mv2[:, t, :], st2[:, t, :])
                            last.then_inc(s_mv2, 1)
                        if slot in NORM2_DVE:
                            dve.wait_ge(s_rstd2, a + 1)
                            if due(a):
                                dve.wait_ge(s_x2_lo, a)
                            t = NORM2_DVE.index(slot)
                            dve.tensor_scalar(x2n[:, t, :], x2[:, t, :], mv2[:, t, 0:1], rstd2[:, t:t + 1], ALU.subtract, ALU.mult)\
                               .then_inc(s_x2n, 1)
                        if slot in X2T_DVE:
                            n = X2T_DVE.index(slot)
                            dve.wait_ge(s_x2T_mm, a * 2 + n + 1)
                            if due(a * FC):
                                dve.wait_ge(s_ffn1_mm, a * FC)
                            dve.tensor_copy(x2T[:, n, :, :].rearrange("p c s -> p (c s)"), x2T_ps)\
                               .then_inc(s_x2T, 1)
                        if slot in H_LO_DVE:
                            low_half(a, LATE_TILES[H_LO_DVE.index(slot)])

            frames(dve, frame)

        @block.tensor
        def _(pe):
            pe.wait_ge(s_pool_set, 2)
            def frame(b, k, par):
                def maxima(u, which):
                    g = b * UNITS + u + 2
                    p = par if u + 2 < UNITS else 1 - par
                    for m in which:
                        qt, i = m // 4, MAX_MAP[m % 4]
                        if u + 2 == UNITS and m == 0:
                            pe.wait_ge(s_q_rows, (b + 2) * 12 * DMA)
                            pe.wait_ge(s_k_rows, (b + 2) * 12 * DMA)
                        if due(g * 16 + m - 1):
                            pe.wait_ge(s_max, g * 16 + m - 1)
                        t, r = 2 * ((u + 2) % UNITS) + i // 2, (i % 2) * HALF
                        pe.matmul(max_ps[m % 2][:, :], q_rows[p][r:r + ROWS, t, qt * P:(qt + 1) * P],
                                  k_rows[p][r:r + ROWS, t, :], start=True, stop=True).then_inc(s_max_mm, 1)

                def scores(u, kt, i, slot):
                    if kt == 0 and i == 0:
                        pe.wait_ge(s_neg_rows, (b * UNITS + u + 1) * MAPS * DMA)
                    if finishes(k) and FFN_AT <= slot < FFN_AT + 3:
                        pe.wait_ge(s_gelu, (b - 1) * FC + (7, 8, 6)[slot - FFN_AT])
                    elif FFN_AT <= slot < FFN_AT + 3:
                        pe.wait_ge(s_exp, b * SLOTS + FFN_AT + (-1, 0, -2)[slot - FFN_AT])
                    else:
                        if due(b * SLOTS + slot - 2):
                            pe.wait_ge(s_exp, b * SLOTS + slot - 2)
                    t, r = 2 * u + SCORE_MAP[i] // 2, (SCORE_MAP[i] % 2) * HALF
                    pe.matmul(score_ps[score_bank(slot)][:, :], k_rows[par][r:r + HALF, t, kt * P:(kt + 1) * P],
                              q_rows[par][r:r + HALF, t, :], start=True, stop=True).then_inc(s_score_mm, 1)

                def value_sums(u, kt, batch, p):
                    n = batch * UNITS + u
                    if kt == 0:
                        if due(n):
                            pe.wait_ge(s_pair, n)
                        if u == 0:
                            pe.wait_ge(s_vals, (batch + 1) * 2)
                    pe.wait_ge(s_exp, (n * STEPS + kt + 1) * MAPS)
                    for i in range(MAPS):
                        last = pe.matmul(pv_ps[i * VW:(i + 1) * VW, :], vals[p][:, kt, 2 * u + i // 2, :],
                                         probs[:, kt % 2, i, :], start=(kt == 0), stop=(kt == STEPS - 1))
                    last.then_inc(s_pv_mm, 1)

                for slot in range(SLOTS):
                    u, kt, i = slot // 16, slot // 4 % 4, slot % 4
                    with_ffn, in_slots = maxima_at(k, u)
                    if slot == FFN_AT and finishes(k):
                        a = b - 1
                        pe.wait_ge(s_x2T, (a + 1) * 2)
                        for j in range(FC):
                            if j < 3:
                                pe.wait_ge(s_exp, b * SLOTS + (FFN_AT + (-1, 0, -2)[j] if attends(k) else 0))
                            else:
                                pe.wait_ge(s_gelu, a * FC + j - 2)
                            for c in range(EC):
                                for n in range(2):
                                    last = pe.matmul(score_ps[ffn_bank(j)][:, :], w1_tern[:, c, j * P:(j + 1) * P],
                                                     x2T[:, n, c, :], start=(c == 0 and n == 0), stop=(c == 1 and n == 1))
                            last.then_inc(s_ffn1_mm, 1)
                            maxima(u, with_ffn[j])
                    if k < 0 and slot == 0:
                        pe.wait_ge(s_w_max, 1)
                        pe.matmul(y_ps[:, 4:5], ones, w_max[:, :], start=True, stop=True).then_inc(s_w_bound, 1)
                    if k < 0 and slot == WTOT_PE:
                        pe.wait_ge(s_wsum, 2)
                        pe.matmul(y_ps[:, 0:2], ones, wsum[:, :], start=True, stop=True).then_inc(s_wtot, 1)
                    if k == 1 and slot == 0:
                        pe.wait_ge(s_const, CONST_LOADS * DMA)
                        pe.wait_ge(s_dve_set, DVE_SET)
                    if slot % 16 in MAX_FIRST:
                        maxima(u, in_slots[slot % 16])
                    if attends(k):
                        scores(u, kt, i, slot)
                    if slot % 16 not in MAX_FIRST:
                        maxima(u, in_slots[slot % 16])
                    if slot % 16 == SUMS_PE[kt]:
                        if kt and attends(k):
                            value_sums(u, kt - 1, b, par)
                        elif not kt and u and attends(k):
                            value_sums(u - 1, STEPS - 1, b, par)
                        elif not kt and not u and attends(k - 1):
                            value_sums(UNITS - 1, STEPS - 1, b - 1, 1 - par)
                    if slot % 16 == OT_PE and has_head(k, u):
                        pe.wait_ge(s_pv_sb, b * UNITS + u)
                        for t in range(NT):
                            last = pe.transpose(pv_ps[:, t * P:(t + 1) * P], pv_sb[:, t * P:(t + 1) * P], ident[:, :])
                        last.then_inc(s_oT_mm, 1)
                    if slot % 16 == NEG_PE and has_neg(k, u):
                        if due(b * UNITS + u + 1):
                            pe.wait_ge(s_neg_sb, b * UNITS + u + 1)
                        if projects(k) and u == 1:
                            pe.wait_ge(s_xT, (b + 2) * 2)
                        if projects(k) and u in (2, 3):
                            pe.wait_ge(s_qk_whole, (b + 1) * 4 + 2 * (u - 1))
                        if projects(k) and (u == 4 or k < 0):
                            pe.wait_ge(s_vals, (b + 2) * 2)
                        pe.wait_ge(s_neg_parts, b * UNITS + u + 2)
                        pe.transpose(neg_ps[:, 0:P], neg_cols[:, :], ident_b[:, :]).then_inc(s_neg_mm, 1)
                    if projects(k):
                        if slot in XT_PE:
                            c = XT_PE.index(slot)
                            if due(b * UNITS + 2):
                                pe.wait_ge(s_neg_sb, b * UNITS + 2)
                            if due((b + 1) * 2 + c):
                                pe.wait_ge(s_xT, (b + 1) * 2 + c)
                            pe.wait_ge((s_x_hi, s_x_lo)[c], (2, 1)[c] * (b + 2))
                            for e in range(EC):
                                for t in range(NT):
                                    at = e * S + t * P
                                    last = pe.transpose(xT_ps[:, at:at + P], xhl[:, c, t, e * P:(e + 1) * P], ident_h[:, :])
                            last.then_inc(s_xT_mm, 1)
                        for n, slots in enumerate(PROJ_PE):
                            if slot not in slots:
                                continue
                            half = slots.index(slot)
                            if half == 0:
                                if due(b * UNITS + 3 + n // 2):
                                    pe.wait_ge(s_neg_sb, b * UNITS + 3 + n // 2)
                                if due((b + 1) * 4 + min(n, 4)):
                                    pe.wait_ge(s_qk_whole, (b + 1) * 4 + min(n, 4))
                                if n == 5:
                                    pe.wait_ge(s_vals, (b + 1) * 2 + 1)
                                if n == 0:
                                    pe.wait_ge(s_xT, (b + 2) * 2)
                                    if k < 0:
                                        pe.wait_ge(s_wqkv_hl, 1)
                            products = ((0, 0), (1, 0), (0, 1))
                            if n < 4:
                                for w, x in products:
                                    last = pe.matmul(x_ps[:, :], wqkv_hl[:, w, half, n * P:(n + 1) * P], xT[:, x, half, :],
                                                     start=(half == 0 and (w, x) == (0, 0)), stop=(half == 1 and (w, x) == (0, 1)))
                            else:
                                t0 = (2 * (n - 4) + half) * P
                                for c in range(EC):
                                    for w, x in products:
                                        last = pe.matmul(x_ps[:, half * E:(half + 1) * E], xT[:, x, c, t0:t0 + P],
                                                         wqkv_hl[:, w, c, 2 * E:3 * E],
                                                         start=(c == 0 and (w, x) == (0, 0)), stop=(c == 1 and (w, x) == (0, 1)))
                            if half:
                                last.then_inc(s_proj_mm, 1)
                    if finishes(k):
                        a = b - 1
                        for h, slots in enumerate(WO_PE):
                            if slot not in slots:
                                continue
                            t = slots.index(slot)
                            if t == 0:
                                if due(a * 2):
                                    pe.wait_ge(s_y, a * 2)
                                if due(a * NT + 2 * h):
                                    pe.wait_ge(s_x2, a * NT + 2 * h)
                                pe.wait_ge(s_heads_n, (a + 1) * UNITS)
                            by_row = heads_n[:, :, :, :, :].rearrange("p c d h f -> p c (d h f)")
                            at = (2 * h + t) * P
                            for c in range(EC):
                                last = pe.matmul(y_ps[:, t * E:(t + 1) * E], by_row[:, c, at:at + P], wo_sb[:, c, :],
                                                 start=(c == 0), stop=(c == 1))
                            if t:
                                last.then_inc(s_wo_mm, 1)
                        if slot in X2T_PE:
                            n = X2T_PE.index(slot)
                            pe.wait_ge(s_x2, (a + 1) * NT)
                            if due(a * 2 + n):
                                pe.wait_ge(s_x2T, a * 2 + n)
                            pe.wait_ge((s_x2_hi, s_x2_lo)[n], (2, 1)[n] * (a + 1))
                            for c in range(EC):
                                for t in range(NT):
                                    at = c * S + t * P
                                    last = pe.transpose(x2T_ps[:, at:at + P], x2hl[:, n, t, c * P:(c + 1) * P], ident_h[:, :])
                            last.then_inc(s_x2T_mm, 1)
                        if slot in FFN2_PE:
                            n = FFN2_PE.index(slot)
                            t, pair_f = FFN2_ORDER[n % 8]
                            at = t * E
                            t += n // 8 * 2
                            if n % 8 == 0:
                                pe.wait_ge(s_x2T, (a + 1) * 2)
                                if due(a * 2 + n // 8):
                                    pe.wait_ge(s_y, a * 2 + n // 8)
                            if n < 2:
                                pe.wait_ge(s_h_lo, a * FC + 2 * n + 2)
                            if n == 4:
                                pe.wait_ge(s_h_lo, (a + 1) * FC)
                            for f in (2 * pair_f, 2 * pair_f + 1):
                                for part in (h_hi, h_lo):
                                    last = pe.matmul(y_ps[:, at:at + E], part[:, f, t * P:(t + 1) * P], w2_tern[:, f, :],
                                                     start=(n % 8 == 0 and f == 0 and part is h_hi),
                                                     stop=(n % 8 == 7 and f == FC - 1 and part is h_lo))
                            if n % 8 == 7:
                                last.then_inc(s_ffn2_mm, 1)

            frames(pe, frame)


_INS = ["x", "w_qkv", "wo", "lq1", "lq2", "lk1", "lk2", "norm_rows", "w1t", "b1c", "b1r", "w2t", "b2r"]


def kernel(L0_attn_x, L0_attn_w_qkv, L0_attn_wo, L0_attn_lambda_q1, L0_attn_lambda_q2, L0_attn_lambda_k1,
           L0_attn_lambda_k2, L0_attn_norm_w, L0_ffn_W1, L0_ffn_b1, L0_ffn_W2, L0_ffn_b2):
    import numpy as _np
    import concourse.bacc as _bacc
    from concourse import mybir as _mybir
    from concourse.bass_utils import run_bass_kernel_spmd as _run

    norm_w = _np.asarray(L0_attn_norm_w)
    by_row = _np.repeat(norm_w.T.reshape(-1), 2).reshape(NT, P).T
    laid = {
        "x": L0_attn_x, "w_qkv": L0_attn_w_qkv, "wo": L0_attn_wo,
        "lq1": L0_attn_lambda_q1, "lq2": L0_attn_lambda_q2, "lk1": L0_attn_lambda_k1, "lk2": L0_attn_lambda_k2,
        "norm_rows": by_row, "w1t": _np.asarray(L0_ffn_W1).T, "b1c": _np.asarray(L0_ffn_b1).reshape(FC, P).T,
        "b1r": L0_ffn_b1, "w2t": _np.asarray(L0_ffn_W2).T, "b2r": L0_ffn_b2,
    }
    nc = _bacc.Bacc("TRN2", target_bir_lowering=False, num_devices=1)
    arrays, args = {}, []
    for name in _INS:
        a = _np.ascontiguousarray(laid[name])
        arrays[f"in_{name}"] = a
        args.append(nc.dram_tensor(f"in_{name}", a.shape, _mybir.dt.from_np(a.dtype), kind="ExternalInput").ap())
    args.append(nc.dram_tensor("out", (B, S, E), F32, kind="ExternalOutput").ap())
    bass_diff_attention_ternary_ffn(nc, *args)
    r = _run(nc, [arrays], core_ids=[0])
    return r.results[0]["out"]
```
